# Optimizing a Trainium2 kernel written in Bass

```python
import numpy as np
import jax
import jax.numpy as jnp

def _softmax(x, axis=-1):
    return jax.nn.softmax(x, axis=axis)

def _gelu(x):
    return jax.nn.gelu(x, approximate=True)

def _silu(x):
    return jax.nn.silu(x)

def _sigmoid(x):
    return jax.nn.sigmoid(x)

def _layernorm(x, axis=-1, eps=1e-05):
    m = jnp.mean(x, axis=axis, keepdims=True)
    v = jnp.var(x, axis=axis, keepdims=True)
    return (x - m) / jnp.sqrt(v + eps)

def _scatter_add(tgt, idx, src, axis=0):
    return tgt.at[idx].add(src)

def _segment_sum(src, seg, n):
    return jax.ops.segment_sum(src, seg, n)
kernel_name = 'mk_pixart_seq_d4_seqx_r8_fa8fad'

def setup_inputs(seed: int=0):
    np.random.seed(seed)
    _w = jnp.asarray

    def _rec_inputs():
        import jax
        import jax.numpy as jnp
        _rk = jax.random.key(seed)
        x = -0.0002928 + 1 * jax.random.normal(jax.random.fold_in(_rk, 1), (128, 64, 128), jnp.float32)
        _lenS = 64 - jax.random.randint(jax.random.fold_in(_rk, 7), (128,), 0, max(1, 64 // 4) + 1, jnp.int32)
        _lenS2 = 64 - jax.random.randint(jax.random.fold_in(_rk, 8), (128,), 0, max(1, 64 // 4) + 1, jnp.int32)
        cond_1024 = 0.0061147 + 1.02565 * jax.random.normal(jax.random.fold_in(_rk, 11), (128, 128), jnp.float32)
        _ctx_1024P = jax.random.normal(jax.random.fold_in(_rk, 12), (128, 16, 128), jnp.float32)
        _ctx_1024c = jax.random.dirichlet(jax.random.fold_in(_rk, 512), 0.3 * jnp.ones((16,), jnp.float32), (128, 64))
        _ctx_1024t = jnp.einsum('bsk,bkd->bsd', _ctx_1024c, _ctx_1024P)
        _ctx_1024t = _ctx_1024t * jax.lax.rsqrt(jnp.mean(jnp.square(_ctx_1024t)) + 1e-12) * 0.953939
        ctx_1024 = -0.00265004 + 0.998804 * (_ctx_1024t + 0.3 * jax.random.normal(jax.random.fold_in(_rk, 612), (128, 64, 128), jnp.float32))
        return (x, cond_1024, ctx_1024)
    x, cond_1024, ctx_1024 = _rec_inputs()

    def _L0_xcond_setup():
        import jax, jax.numpy as jnp
        import numpy as np
        D = 128
        H = 16
        HD = D // H
        MLP = 4 * D
        EPS = 1e-06
        SCALE = HD ** (-0.5)

        def _p(key, shape, s=0.02):
            return jax.random.normal(key, shape, dtype=jnp.float32) * s

        def _ln(x):
            mu = jnp.mean(x, axis=-1, keepdims=True)
            var = jnp.var(x, axis=-1, keepdims=True)
            return (x - mu) * jax.lax.rsqrt(var + EPS)

        def _heads(t):
            B, L, _ = t.shape
            return t.reshape(B, L, H, HD).transpose(0, 2, 1, 3)

        def _attend(q, k, v):
            attn = jnp.einsum('bhnd,bhsd->bhns', q, k) * SCALE
            attn = jax.nn.softmax(attn, axis=-1)
            o = jnp.einsum('bhns,bhsd->bhnd', attn, v)
            B, _, N, _ = q.shape
            return o.transpose(0, 2, 1, 3).reshape(B, N, D)
        key = jax.random.key(seed)
        ks = jax.random.split(key, 24)
        B, N, S = (4, 128, 77)
        return {'x': jax.random.normal(ks[0], (B, N, D), dtype=jnp.float32), 't_emb': jax.random.normal(ks[1], (B, D), dtype=jnp.float32), 'context': jax.random.normal(ks[2], (B, S, D), dtype=jnp.float32), 'adaln_w': _p(ks[3], (D, 6 * D)), 'adaln_b': _p(ks[4], (6 * D,)), 'qkv_w': _p(ks[5], (D, 3 * D)), 'qkv_b': _p(ks[6], (3 * D,)), 'sa_proj_w': _p(ks[7], (D, D)), 'sa_proj_b': _p(ks[8], (D,)), 'q_w': _p(ks[9], (D, D)), 'q_b': _p(ks[10], (D,)), 'kv_w': _p(ks[11], (D, 2 * D)), 'kv_b': _p(ks[12], (2 * D,)), 'ca_proj_w': _p(ks[13], (D, D)), 'ca_proj_b': _p(ks[14], (D,)), 'fc1_w': _p(ks[15], (D, MLP)), 'fc1_b': _p(ks[16], (MLP,)), 'fc2_w': _p(ks[17], (MLP, D)), 'fc2_b': _p(ks[18], (D,))}
    _L0_xcond_all = _L0_xcond_setup()
    _L0_xcond_in = {k: v for k, v in _L0_xcond_all.items() if k in ('adaln_w', 'adaln_b', 'qkv_w', 'qkv_b', 'sa_proj_w', 'sa_proj_b', 'q_w', 'q_b', 'kv_w', 'kv_b', 'ca_proj_w', 'ca_proj_b', 'fc1_w', 'fc1_b', 'fc2_w', 'fc2_b')}
    del _L0_xcond_all

    def _L1_xcond_setup():
        import jax, jax.numpy as jnp
        import numpy as np
        EPS = 1e-05

        def _ada_ln(x, c, W_ss, b_ss):
            mu = jnp.mean(x, axis=-1, keepdims=True)
            var = jnp.mean((x - mu) ** 2, axis=-1, keepdims=True)
            h = (x - mu) / jnp.sqrt(var + EPS)
            ss = jax.nn.silu(c) @ W_ss + b_ss
            scale, bias = jnp.split(ss, 2, axis=-1)
            return (1.0 + scale)[:, None, :] * h + bias[:, None, :]
        key = jax.random.key(seed)
        ks = jax.random.split(key, 12)
        B, Lq, Lkv, H = (8, 256, 64, 128)
        s = 0.02
        return {'x_q': jax.random.normal(ks[0], (B, Lq, H), jnp.float32), 'x_kv': jax.random.normal(ks[1], (B, Lkv, H), jnp.float32), 't_vec': jax.random.normal(ks[2], (B, H), jnp.float32), 'Wq': jax.random.normal(ks[3], (H, H), jnp.float32) * s, 'bq': jnp.zeros((H,), jnp.float32), 'Wkv': jax.random.normal(ks[4], (H, 2 * H), jnp.float32) * s, 'bkv': jnp.zeros((2 * H,), jnp.float32), 'Wp': jax.random.normal(ks[5], (H, H), jnp.float32) * s, 'bp': jnp.zeros((H,), jnp.float32), 'Wss_q': jax.random.normal(ks[6], (H, 2 * H), jnp.float32) * s, 'bss_q': jnp.zeros((2 * H,), jnp.float32), 'Wss_kv': jax.random.normal(ks[7], (H, 2 * H), jnp.float32) * s, 'bss_kv': jnp.zeros((2 * H,), jnp.float32)}
    _L1_xcond_all = _L1_xcond_setup()
    _L1_xcond_in = {k: v for k, v in _L1_xcond_all.items() if k in ('Wq', 'bq', 'Wkv', 'bkv', 'Wp', 'bp', 'Wss_q', 'bss_q', 'Wss_kv', 'bss_kv')}
    del _L1_xcond_all

    def _L2_xcond_setup():
        import jax, jax.numpy as jnp
        import numpy as np
        LN_EPS = 1e-06

        def _ln(x):
            mu = jnp.mean(x, axis=-1, keepdims=True)
            var = jnp.var(x, axis=-1, keepdims=True)
            return (x - mu) * jax.lax.rsqrt(var + LN_EPS)
        key = jax.random.key(seed)
        H, NH = (128, 16)
        B, N, S = (4, 128, 77)
        MLP = int(H * 4.0)
        ks = jax.random.split(key, 20)
        s = 1.0 / np.sqrt(H)
        return {'x': jax.random.normal(ks[0], (B, N, H), jnp.float32), 'c': jax.random.normal(ks[1], (B, H), jnp.float32), 'context': jax.random.normal(ks[2], (B, S, H), jnp.float32), 'W_mod': jax.random.normal(ks[3], (H, 6 * H), jnp.float32) * s, 'b_mod': jnp.zeros((6 * H,), jnp.float32), 'W_qkv': jax.random.normal(ks[4], (H, 3 * H), jnp.float32) * s, 'b_qkv': jnp.zeros((3 * H,), jnp.float32), 'W_proj': jax.random.normal(ks[5], (H, H), jnp.float32) * s, 'b_proj': jnp.zeros((H,), jnp.float32), 'W_qc': jax.random.normal(ks[6], (H, H), jnp.float32) * s, 'b_qc': jnp.zeros((H,), jnp.float32), 'W_kvc': jax.random.normal(ks[7], (H, 2 * H), jnp.float32) * s, 'b_kvc': jnp.zeros((2 * H,), jnp.float32), 'W_cproj': jax.random.normal(ks[8], (H, H), jnp.float32) * s, 'b_cproj': jnp.zeros((H,), jnp.float32), 'W_mlp1': jax.random.normal(ks[9], (H, MLP), jnp.float32) * s, 'b_mlp1': jnp.zeros((MLP,), jnp.float32), 'W_mlp2': jax.random.normal(ks[10], (MLP, H), jnp.float32) * (1.0 / np.sqrt(MLP)), 'b_mlp2': jnp.zeros((H,), jnp.float32)}
    _L2_xcond_all = _L2_xcond_setup()
    _L2_xcond_in = {k: v for k, v in _L2_xcond_all.items() if k in ('W_mod', 'b_mod', 'W_qkv', 'b_qkv', 'W_proj', 'b_proj', 'W_qc', 'b_qc', 'W_kvc', 'b_kvc', 'W_cproj', 'b_cproj', 'W_mlp1', 'b_mlp1', 'W_mlp2', 'b_mlp2')}
    del _L2_xcond_all

    def _L3_xcond_setup():
        import jax, jax.numpy as jnp
        import numpy as np
        H = 128
        RH = 2 * H
        E = 3
        B, T, P = (8, 256, 64)
        LN_EPS = 1e-05

        def _layer_norm(x, gamma, beta):
            mu = jnp.mean(x, axis=-1, keepdims=True)
            var = jnp.mean(jnp.square(x - mu), axis=-1, keepdims=True)
            return (x - mu) * jax.lax.rsqrt(var + LN_EPS) * gamma + beta
        key = jax.random.key(seed)
        ks = jax.random.split(key, 24)
        s = lambda fan_in: 1.0 / np.sqrt(fan_in)
        inp = {'mix_hidden_states': jax.random.normal(ks[0], (B, T, H), jnp.float32), 'global_anchor': jax.random.normal(ks[1], (B, H), jnp.float32), 'prototype_bank': jax.random.normal(ks[2], (B, P, H), jnp.float32), 'ln_gamma': jnp.ones((H,), jnp.float32), 'ln_beta': jnp.zeros((H,), jnp.float32), 'Wq': jax.random.normal(ks[3], (H, H), jnp.float32) * s(H), 'Wk': jax.random.normal(ks[4], (H, H), jnp.float32) * s(H), 'Wv': jax.random.normal(ks[5], (H, H), jnp.float32) * s(H), 'router_W': jax.random.normal(ks[6], (3 * H, E), jnp.float32) * s(3 * H), 'router_b': jnp.zeros((E,), jnp.float32), 'e_w1': jax.random.normal(ks[7], (E, 3 * H, RH), jnp.float32) * s(3 * H), 'e_b1': jnp.zeros((E, RH), jnp.float32), 'e_w2': jax.random.normal(ks[8], (E, RH, H), jnp.float32) * s(RH), 'e_b2': jnp.zeros((E, H), jnp.float32), 'gate_w1': jax.random.normal(ks[9], (3 * H, H), jnp.float32) * s(3 * H), 'gate_b1': jnp.zeros((H,), jnp.float32), 'gate_w2': jax.random.normal(ks[10], (H, H), jnp.float32) * s(H), 'gate_b2': jnp.zeros((H,), jnp.float32), 'out_w': jax.random.normal(ks[11], (H, H), jnp.float32) * s(H), 'out_b': jnp.zeros((H,), jnp.float32)}
        return inp
    _L3_xcond_all = _L3_xcond_setup()
    _L3_xcond_in = {k: v for k, v in _L3_xcond_all.items() if k in ('ln_gamma', 'ln_beta', 'Wq', 'Wk', 'Wv', 'router_W', 'router_b', 'e_w1', 'e_b1', 'e_w2', 'e_b2', 'gate_w1', 'gate_b1', 'gate_w2', 'gate_b2', 'out_w', 'out_b')}
    del _L3_xcond_all
    return {'x': x, 'cond_1024': cond_1024, 'ctx_1024': ctx_1024, 'L0_xcond_adaln_w': _L0_xcond_in['adaln_w'], 'L0_xcond_adaln_b': _L0_xcond_in['adaln_b'], 'L0_xcond_qkv_w': _L0_xcond_in['qkv_w'], 'L0_xcond_qkv_b': _L0_xcond_in['qkv_b'], 'L0_xcond_sa_proj_w': _L0_xcond_in['sa_proj_w'], 'L0_xcond_sa_proj_b': _L0_xcond_in['sa_proj_b'], 'L0_xcond_q_w': _L0_xcond_in['q_w'], 'L0_xcond_q_b': _L0_xcond_in['q_b'], 'L0_xcond_kv_w': _L0_xcond_in['kv_w'], 'L0_xcond_kv_b': _L0_xcond_in['kv_b'], 'L0_xcond_ca_proj_w': _L0_xcond_in['ca_proj_w'], 'L0_xcond_ca_proj_b': _L0_xcond_in['ca_proj_b'], 'L0_xcond_fc1_w': _L0_xcond_in['fc1_w'], 'L0_xcond_fc1_b': _L0_xcond_in['fc1_b'], 'L0_xcond_fc2_w': _L0_xcond_in['fc2_w'], 'L0_xcond_fc2_b': _L0_xcond_in['fc2_b'], 'L1_xcond_Wq': _L1_xcond_in['Wq'], 'L1_xcond_bq': _L1_xcond_in['bq'], 'L1_xcond_Wkv': _L1_xcond_in['Wkv'], 'L1_xcond_bkv': _L1_xcond_in['bkv'], 'L1_xcond_Wp': _L1_xcond_in['Wp'], 'L1_xcond_bp': _L1_xcond_in['bp'], 'L1_xcond_Wss_q': _L1_xcond_in['Wss_q'], 'L1_xcond_bss_q': _L1_xcond_in['bss_q'], 'L1_xcond_Wss_kv': _L1_xcond_in['Wss_kv'], 'L1_xcond_bss_kv': _L1_xcond_in['bss_kv'], 'L2_xcond_W_mod': _L2_xcond_in['W_mod'], 'L2_xcond_b_mod': _L2_xcond_in['b_mod'], 'L2_xcond_W_qkv': _L2_xcond_in['W_qkv'], 'L2_xcond_b_qkv': _L2_xcond_in['b_qkv'], 'L2_xcond_W_proj': _L2_xcond_in['W_proj'], 'L2_xcond_b_proj': _L2_xcond_in['b_proj'], 'L2_xcond_W_qc': _L2_xcond_in['W_qc'], 'L2_xcond_b_qc': _L2_xcond_in['b_qc'], 'L2_xcond_W_kvc': _L2_xcond_in['W_kvc'], 'L2_xcond_b_kvc': _L2_xcond_in['b_kvc'], 'L2_xcond_W_cproj': _L2_xcond_in['W_cproj'], 'L2_xcond_b_cproj': _L2_xcond_in['b_cproj'], 'L2_xcond_W_mlp1': _L2_xcond_in['W_mlp1'], 'L2_xcond_b_mlp1': _L2_xcond_in['b_mlp1'], 'L2_xcond_W_mlp2': _L2_xcond_in['W_mlp2'], 'L2_xcond_b_mlp2': _L2_xcond_in['b_mlp2'], 'L3_xcond_ln_gamma': _L3_xcond_in['ln_gamma'], 'L3_xcond_ln_beta': _L3_xcond_in['ln_beta'], 'L3_xcond_Wq': _L3_xcond_in['Wq'], 'L3_xcond_Wk': _L3_xcond_in['Wk'], 'L3_xcond_Wv': _L3_xcond_in['Wv'], 'L3_xcond_router_W': _L3_xcond_in['router_W'], 'L3_xcond_router_b': _L3_xcond_in['router_b'], 'L3_xcond_e_w1': _L3_xcond_in['e_w1'], 'L3_xcond_e_b1': _L3_xcond_in['e_b1'], 'L3_xcond_e_w2': _L3_xcond_in['e_w2'], 'L3_xcond_e_b2': _L3_xcond_in['e_b2'], 'L3_xcond_gate_w1': _L3_xcond_in['gate_w1'], 'L3_xcond_gate_b1': _L3_xcond_in['gate_b1'], 'L3_xcond_gate_w2': _L3_xcond_in['gate_w2'], 'L3_xcond_gate_b2': _L3_xcond_in['gate_b2'], 'L3_xcond_out_w': _L3_xcond_in['out_w'], 'L3_xcond_out_b': _L3_xcond_in['out_b']}

def reference(x, cond_1024, ctx_1024, L0_xcond_adaln_w, L0_xcond_adaln_b, L0_xcond_qkv_w, L0_xcond_qkv_b, L0_xcond_sa_proj_w, L0_xcond_sa_proj_b, L0_xcond_q_w, L0_xcond_q_b, L0_xcond_kv_w, L0_xcond_kv_b, L0_xcond_ca_proj_w, L0_xcond_ca_proj_b, L0_xcond_fc1_w, L0_xcond_fc1_b, L0_xcond_fc2_w, L0_xcond_fc2_b, L1_xcond_Wq, L1_xcond_bq, L1_xcond_Wkv, L1_xcond_bkv, L1_xcond_Wp, L1_xcond_bp, L1_xcond_Wss_q, L1_xcond_bss_q, L1_xcond_Wss_kv, L1_xcond_bss_kv, L2_xcond_W_mod, L2_xcond_b_mod, L2_xcond_W_qkv, L2_xcond_b_qkv, L2_xcond_W_proj, L2_xcond_b_proj, L2_xcond_W_qc, L2_xcond_b_qc, L2_xcond_W_kvc, L2_xcond_b_kvc, L2_xcond_W_cproj, L2_xcond_b_cproj, L2_xcond_W_mlp1, L2_xcond_b_mlp1, L2_xcond_W_mlp2, L2_xcond_b_mlp2, L3_xcond_ln_gamma, L3_xcond_ln_beta, L3_xcond_Wq, L3_xcond_Wk, L3_xcond_Wv, L3_xcond_router_W, L3_xcond_router_b, L3_xcond_e_w1, L3_xcond_e_b1, L3_xcond_e_w2, L3_xcond_e_b2, L3_xcond_gate_w1, L3_xcond_gate_b1, L3_xcond_gate_w2, L3_xcond_gate_b2, L3_xcond_out_w, L3_xcond_out_b):
    import jax
    import jax.numpy as jnp

    def _L0_xcond_ref(x, t_emb, context, adaln_w, adaln_b, qkv_w, qkv_b, sa_proj_w, sa_proj_b, q_w, q_b, kv_w, kv_b, ca_proj_w, ca_proj_b, fc1_w, fc1_b, fc2_w, fc2_b):
        import jax, jax.numpy as jnp
        import numpy as np
        D = 128
        H = 16
        HD = D // H
        MLP = 4 * D
        EPS = 1e-06
        SCALE = HD ** (-0.5)

        def _p(key, shape, s=0.02):
            return jax.random.normal(key, shape, dtype=jnp.float32) * s

        def _ln(x):
            mu = jnp.mean(x, axis=-1, keepdims=True)
            var = jnp.var(x, axis=-1, keepdims=True)
            return (x - mu) * jax.lax.rsqrt(var + EPS)

        def _heads(t):
            B, L, _ = t.shape
            return t.reshape(B, L, H, HD).transpose(0, 2, 1, 3)

        def _attend(q, k, v):
            attn = jnp.einsum('bhnd,bhsd->bhns', q, k) * SCALE
            attn = jax.nn.softmax(attn, axis=-1)
            o = jnp.einsum('bhns,bhsd->bhnd', attn, v)
            B, _, N, _ = q.shape
            return o.transpose(0, 2, 1, 3).reshape(B, N, D)
        B, N, _ = x.shape
        S = context.shape[1]
        mod = jax.nn.silu(t_emb) @ adaln_w + adaln_b
        sh_sa, sc_sa, g_sa, sh_ff, sc_ff, g_ff = jnp.split(mod[:, None, :], 6, axis=-1)
        xm = _ln(x) * (1.0 + sc_sa) + sh_sa
        qkv = (xm @ qkv_w + qkv_b).reshape(B, N, 3, H, HD)
        q = qkv[:, :, 0].transpose(0, 2, 1, 3)
        k = qkv[:, :, 1].transpose(0, 2, 1, 3)
        v = qkv[:, :, 2].transpose(0, 2, 1, 3)
        x_sa = _attend(q, k, v) @ sa_proj_w + sa_proj_b
        x = x + g_sa * x_sa
        xn = _ln(x)
        q = _heads(xn @ q_w + q_b)
        kv = (context @ kv_w + kv_b).reshape(B, S, 2, H, HD)
        k = kv[:, :, 0].transpose(0, 2, 1, 3)
        v = kv[:, :, 1].transpose(0, 2, 1, 3)
        x_ca = _attend(q, k, v) @ ca_proj_w + ca_proj_b
        x = x + x_ca
        xm = _ln(x) * (1.0 + sc_ff) + sh_ff
        h = jax.nn.gelu(xm @ fc1_w + fc1_b, approximate=True)
        x_ff = h @ fc2_w + fc2_b
        x = x + g_ff * x_ff
        return x

    def _L1_xcond_ref(x_q, x_kv, t_vec, Wq, bq, Wkv, bkv, Wp, bp, Wss_q, bss_q, Wss_kv, bss_kv):
        import jax, jax.numpy as jnp
        import numpy as np
        EPS = 1e-05

        def _ada_ln(x, c, W_ss, b_ss):
            mu = jnp.mean(x, axis=-1, keepdims=True)
            var = jnp.mean((x - mu) ** 2, axis=-1, keepdims=True)
            h = (x - mu) / jnp.sqrt(var + EPS)
            ss = jax.nn.silu(c) @ W_ss + b_ss
            scale, bias = jnp.split(ss, 2, axis=-1)
            return (1.0 + scale)[:, None, :] * h + bias[:, None, :]
        B, Lq, H = x_q.shape
        Lkv = x_kv.shape[1]
        nh = 16
        dh = H // nh
        xq = _ada_ln(x_q, t_vec, Wss_q, bss_q)
        xkv = _ada_ln(x_kv, t_vec, Wss_kv, bss_kv)
        q = (xq @ Wq + bq).reshape(B, Lq, nh, dh)
        kv = (xkv @ Wkv + bkv).reshape(B, Lkv, 2, nh, dh)
        k = kv[:, :, 0]
        v = kv[:, :, 1]
        scores = jnp.einsum('bqhd,bkhd->bhqk', q, k) / jnp.sqrt(jnp.float32(dh))
        attn = jax.nn.softmax(scores, axis=-1)
        out = jnp.einsum('bhqk,bkhd->bqhd', attn, v).reshape(B, Lq, H)
        return x_q + (out @ Wp + bp)

    def _L2_xcond_ref(x, c, context, W_mod, b_mod, W_qkv, b_qkv, W_proj, b_proj, W_qc, b_qc, W_kvc, b_kvc, W_cproj, b_cproj, W_mlp1, b_mlp1, W_mlp2, b_mlp2):
        import jax, jax.numpy as jnp
        import numpy as np
        LN_EPS = 1e-06

        def _ln(x):
            mu = jnp.mean(x, axis=-1, keepdims=True)
            var = jnp.var(x, axis=-1, keepdims=True)
            return (x - mu) * jax.lax.rsqrt(var + LN_EPS)
        B, N, H = x.shape
        NH = 16
        hd = H // NH
        scale = hd ** (-0.5)
        c_proj = jax.nn.silu(c) @ W_mod + b_mod
        shift_a, scale_a, gate_a, shift_m, scale_m, gate_m = jnp.split(c_proj, 6, axis=-1)

        def modulate(t, shift, sc):
            return t * (1 + sc[:, None]) + shift[:, None]
        x_norm = modulate(_ln(x), shift_a, scale_a)
        qkv = x_norm @ W_qkv + b_qkv
        q, k, v = jnp.split(qkv, 3, axis=-1)
        q = q.reshape(B, N, NH, hd).transpose(0, 2, 1, 3)
        k = k.reshape(B, N, NH, hd).transpose(0, 2, 1, 3)
        v = v.reshape(B, N, NH, hd).transpose(0, 2, 1, 3)
        attn_w = jax.nn.softmax(jnp.einsum('bhqd,bhkd->bhqk', q, k) * scale, axis=-1)
        attn_out = jnp.einsum('bhqk,bhkd->bhqd', attn_w, v)
        attn_out = attn_out.transpose(0, 2, 1, 3).reshape(B, N, H)
        attn_out = attn_out @ W_proj + b_proj
        x = x + gate_a[:, None] * attn_out
        S = context.shape[1]
        q_c = _ln(x) @ W_qc + b_qc
        kv_c = _ln(context) @ W_kvc + b_kvc
        k_c, v_c = jnp.split(kv_c, 2, axis=-1)
        q_c = q_c.reshape(B, N, NH, hd).transpose(0, 2, 1, 3)
        k_c = k_c.reshape(B, S, NH, hd).transpose(0, 2, 1, 3)
        v_c = v_c.reshape(B, S, NH, hd).transpose(0, 2, 1, 3)
        c_attn_w = jax.nn.softmax(jnp.einsum('bhqd,bhsd->bhqs', q_c, k_c) * scale, axis=-1)
        c_attn_out = jnp.einsum('bhqs,bhsd->bhqd', c_attn_w, v_c)
        c_attn_out = c_attn_out.transpose(0, 2, 1, 3).reshape(B, N, H)
        c_attn_out = c_attn_out @ W_cproj + b_cproj
        x = x + c_attn_out
        x_norm2 = modulate(_ln(x), shift_m, scale_m)
        h = jax.nn.gelu(x_norm2 @ W_mlp1 + b_mlp1)
        h = h @ W_mlp2 + b_mlp2
        x = x + gate_m[:, None] * h
        return x

    def _L3_xcond_ref(mix_hidden_states, global_anchor, prototype_bank, ln_gamma, ln_beta, Wq, Wk, Wv, router_W, router_b, e_w1, e_b1, e_w2, e_b2, gate_w1, gate_b1, gate_w2, gate_b2, out_w, out_b):
        import jax, jax.numpy as jnp
        import numpy as np
        H = 128
        RH = 2 * H
        E = 3
        B, T, P = (8, 256, 64)
        LN_EPS = 1e-05

        def _layer_norm(x, gamma, beta):
            mu = jnp.mean(x, axis=-1, keepdims=True)
            var = jnp.mean(jnp.square(x - mu), axis=-1, keepdims=True)
            return (x - mu) * jax.lax.rsqrt(var + LN_EPS) * gamma + beta
        x = mix_hidden_states
        nx = _layer_norm(x, ln_gamma, ln_beta)
        q = nx @ Wq
        k = prototype_bank @ Wk
        v = prototype_bank @ Wv
        scores = jnp.einsum('bth,bph->btp', q, k) * H ** (-0.5)
        weights = jax.nn.softmax(scores, axis=-1)
        evidence = jnp.einsum('btp,bph->bth', weights, v)
        anchor = jnp.broadcast_to(global_anchor[:, None, :], nx.shape)
        combined = jnp.concatenate([nx, evidence, anchor], axis=-1)
        router_logits = combined @ router_W + router_b
        router_probs = jax.nn.softmax(router_logits, axis=-1)
        h = jax.nn.silu(jnp.einsum('btc,ecr->bter', combined, e_w1) + e_b1)
        expert_out = jnp.einsum('bter,erh->bteh', h, e_w2) + e_b2
        routed = jnp.sum(expert_out * router_probs[..., None], axis=-2)
        g = jax.nn.sigmoid(jax.nn.silu(combined @ gate_w1 + gate_b1) @ gate_w2 + gate_b2)
        refined_delta = g * (routed @ out_w + out_b)
        return x + refined_delta
    x = _L0_xcond_ref(x, cond_1024, ctx_1024, L0_xcond_adaln_w, L0_xcond_adaln_b, L0_xcond_qkv_w, L0_xcond_qkv_b, L0_xcond_sa_proj_w, L0_xcond_sa_proj_b, L0_xcond_q_w, L0_xcond_q_b, L0_xcond_kv_w, L0_xcond_kv_b, L0_xcond_ca_proj_w, L0_xcond_ca_proj_b, L0_xcond_fc1_w, L0_xcond_fc1_b, L0_xcond_fc2_w, L0_xcond_fc2_b)
    x = _L1_xcond_ref(x, ctx_1024, cond_1024, L1_xcond_Wq, L1_xcond_bq, L1_xcond_Wkv, L1_xcond_bkv, L1_xcond_Wp, L1_xcond_bp, L1_xcond_Wss_q, L1_xcond_bss_q, L1_xcond_Wss_kv, L1_xcond_bss_kv)
    x = _L2_xcond_ref(x, cond_1024, ctx_1024, L2_xcond_W_mod, L2_xcond_b_mod, L2_xcond_W_qkv, L2_xcond_b_qkv, L2_xcond_W_proj, L2_xcond_b_proj, L2_xcond_W_qc, L2_xcond_b_qc, L2_xcond_W_kvc, L2_xcond_b_kvc, L2_xcond_W_cproj, L2_xcond_b_cproj, L2_xcond_W_mlp1, L2_xcond_b_mlp1, L2_xcond_W_mlp2, L2_xcond_b_mlp2)
    x = _L3_xcond_ref(x, cond_1024, ctx_1024, L3_xcond_ln_gamma, L3_xcond_ln_beta, L3_xcond_Wq, L3_xcond_Wk, L3_xcond_Wv, L3_xcond_router_W, L3_xcond_router_b, L3_xcond_e_w1, L3_xcond_e_b1, L3_xcond_e_w2, L3_xcond_e_b2, L3_xcond_gate_w1, L3_xcond_gate_b1, L3_xcond_gate_w2, L3_xcond_gate_b2, L3_xcond_out_w, L3_xcond_out_b)
    return x

_drawn_inputs = setup_inputs


def setup_inputs(seed=0):
    import zlib

    import numpy as np

    out = dict(_drawn_inputs(seed))
    spreads = {'L1_xcond_bq': (0.0, 2.0),
     'L1_xcond_bkv': (0.0, 2.0),
     'L1_xcond_bp': (0.0, 0.758),
     'L1_xcond_bss_q': (0.0, 2.0),
     'L1_xcond_bss_kv': (0.0, 2.0),
     'L2_xcond_b_mod': (0.0, 0.418),
     'L2_xcond_b_qkv': (0.0, 0.8),
     'L2_xcond_b_proj': (0.0, 0.8),
     'L2_xcond_b_qc': (0.0, 2.0),
     'L2_xcond_b_kvc': (0.0, 0.765),
     'L2_xcond_b_cproj': (0.0, 0.751),
     'L2_xcond_b_mlp1': (0.0, 2.0),
     'L2_xcond_b_mlp2': (0.0, 0.8),
     'L3_xcond_ln_gamma': (1.0, 0.6),
     'L3_xcond_ln_beta': (0.0, 2.0),
     'L3_xcond_router_b': (0.0, 2.0),
     'L3_xcond_e_b1': (0.0, 2.0),
     'L3_xcond_e_b2': (0.0, 1.793),
     'L3_xcond_gate_b1': (0.0, 2.0),
     'L3_xcond_gate_b2': (0.0, 2.0),
     'L3_xcond_out_b': (0.0, 2.0)}
    factors = {'L0_xcond_adaln_w': 6.921,
     'L0_xcond_adaln_b': 8.0,
     'L0_xcond_qkv_w': 8.0,
     'L0_xcond_qkv_b': 8.0,
     'L0_xcond_sa_proj_w': 8.0,
     'L0_xcond_sa_proj_b': 8.0,
     'L0_xcond_q_w': 64.0,
     'L0_xcond_q_b': 64.0,
     'L0_xcond_kv_b': 64.0,
     'L0_xcond_ca_proj_b': 16.852,
     'L0_xcond_fc1_w': 8.0,
     'L0_xcond_fc1_b': 8.0,
     'L0_xcond_fc2_w': 8.0,
     'L0_xcond_fc2_b': 27.669,
     'L1_xcond_Wq': 64.0,
     'L1_xcond_Wss_q': 64.0,
     'L1_xcond_Wss_kv': 51.504,
     'L0_xcond_kv_w': 8.0,
     'L0_xcond_ca_proj_w': 7.454,
     'L1_xcond_Wkv': 6.839,
     'L1_xcond_Wp': 4.665,
     'L2_xcond_W_qc': 2.821,
     'L3_xcond_Wq': 8.0,
     'L3_xcond_Wk': 8.0,
     'L3_xcond_Wv': 4.793,
     'L3_xcond_router_W': 2.994,
     'L3_xcond_gate_w1': 6.815,
     'L3_xcond_gate_w2': 5.185}
    for name, (base, spread) in spreads.items():
        noise = np.random.default_rng([zlib.crc32(name.encode()), seed]).standard_normal(out[name].shape)
        drawn = base * np.exp(spread * noise) if base else spread * noise
        out[name] = jnp.asarray(drawn.astype(out[name].dtype))
    for name, factor in factors.items():
        out[name] = (out[name] * factor).astype(out[name].dtype)
    return out
```

```python
from contextlib import ExitStack

import numpy as np

import concourse.bass as bass
from concourse import mybir

ALU = mybir.AluOpType
ACT = mybir.ActivationFunctionType
AX = mybir.AxisListType
F32 = mybir.dt.float32
ENGINES = [mybir.EngineType.Pool, mybir.EngineType.Activation, mybir.EngineType.PE,
           mybir.EngineType.DVE, mybir.EngineType.SP]

D = 128
HEADS = 16
HD = D // HEADS
SEQ = 64
GROUP = 4
TOK = GROUP * SEQ
STREAMS = 4
TURNS = HEADS // 4
EXPERTS = 3

WEIGHTS = {
    "L0_adaln_w": (1, 768), "L1_Wss_q": (1, 256), "L1_Wss_kv": (1, 256), "L2_W_mod": (1, 768),
    "L0_qkv_w": (1, 384), "L0_sa_proj_w": (1, 128), "L0_q_w": (1, 128), "L0_kv_w": (1, 256),
    "L0_ca_proj_w": (1, 128), "L0_fc1_w": (1, 512), "L0_fc2_w": (4, 128),
    "L1_Wq": (1, 128), "L1_Wkv": (1, 256), "L1_Wp": (1, 128),
    "L2_W_qkv": (1, 384), "L2_W_proj": (1, 128), "L2_W_qc": (1, 128), "L2_W_kvc": (1, 256),
    "L2_W_cproj": (1, 128), "L2_W_mlp1": (1, 512), "L2_W_mlp2": (4, 128),
    "L3_Wq": (1, 128), "L3_Wk": (1, 128), "L3_Wv": (1, 128), "L3_router_W": (3, 3),
    "L3_e_w1": (9, 256), "L3_e_w2": (6, 128), "L3_gate_w1": (3, 128), "L3_gate_w2": (1, 128),
    "L3_out_w": (1, 128),
}
BIASES = {
    "L0_adaln_b": 6, "L1_bss_q": 2, "L1_bss_kv": 2, "L2_b_mod": 6,
    "L0_qkv_b": 3, "L0_sa_proj_b": 1, "L0_q_b": 1, "L0_kv_b": 2, "L0_ca_proj_b": 1, "L0_fc1_b": 4,
    "L0_fc2_b": 1, "L1_bq": 1, "L1_bkv": 2, "L1_bp": 1,
    "L2_b_qkv": 3, "L2_b_proj": 1, "L2_b_qc": 1, "L2_b_kvc": 2, "L2_b_cproj": 1, "L2_b_mlp1": 4,
    "L2_b_mlp2": 1, "L3_ln_gamma": 1, "L3_ln_beta": 1, "L3_e_b1": 6, "L3_gate_b1": 1,
    "L3_gate_b2": 1, "L3_out_b": 1,
}


def offsets(table, width):
    at, out = 0, {}
    for name, size in table.items():
        out[name] = at
        at += width(size)
    return out, at


W_AT, W_COLS = offsets(WEIGHTS, lambda s: s[0] * s[1])
B_AT, B_COLS = offsets(BIASES, lambda s: s)

MODS = (
    [("L0_adaln_w", 0, c, "L0_adaln_b", c, c in (1, 4)) for c in range(6)]
    + [("L1_Wss_q", 0, c, "L1_bss_q", c, c == 0) for c in range(2)]
    + [("L1_Wss_kv", 0, c, "L1_bss_kv", c, c == 0) for c in range(2)]
    + [("L2_W_mod", 0, c, "L2_b_mod", c, c in (1, 4)) for c in range(6)]
)
M_L0, M_L1Q, M_L1KV, M_L2 = 0, 6, 8, 10
M_EXPERT = len(MODS)
M_GATE = M_EXPERT + 2 * EXPERTS
M_COND = M_GATE + 1
N_MODS = M_COND + 1

ATT_SCALE = float(HD) ** -0.5
L3_SCALE = float(D) ** -0.5
O_COLS = 2 * (HD + 1)

SELF0 = dict(kv="n", wq=("L0_qkv_w", 0), wk=("L0_qkv_w", 1), wv=("L0_qkv_w", 2), bq=("L0_qkv_b", 0),
             bk=("L0_qkv_b", 1), bv=("L0_qkv_b", 2), wp="L0_sa_proj_w", bp="L0_sa_proj_b", gate=M_L0 + 2)
CROSS0 = dict(kv="ctx", wq=("L0_q_w", 0), wk=("L0_kv_w", 0), wv=("L0_kv_w", 1), bq=("L0_q_b", 0),
              bk=("L0_kv_b", 0), bv=("L0_kv_b", 1), wp="L0_ca_proj_w", bp="L0_ca_proj_b", gate=None)
CROSS1 = dict(kv="kvn", wq=("L1_Wq", 0), wk=("L1_Wkv", 0), wv=("L1_Wkv", 1), bq=("L1_bq", 0),
              bk=("L1_bkv", 0), bv=("L1_bkv", 1), wp="L1_Wp", bp="L1_bp", gate=None)
SELF2 = dict(kv="n", wq=("L2_W_qkv", 0), wk=("L2_W_qkv", 1), wv=("L2_W_qkv", 2), bq=("L2_b_qkv", 0),
             bk=("L2_b_qkv", 1), bv=("L2_b_qkv", 2), wp="L2_W_proj", bp="L2_b_proj", gate=M_L2 + 2)
CROSS2 = dict(kv="kvn", wq=("L2_W_qc", 0), wk=("L2_W_kvc", 0), wv=("L2_W_kvc", 1), bq=("L2_b_qc", 0),
              bk=("L2_b_kvc", 0), bv=("L2_b_kvc", 1), wp="L2_W_cproj", bp="L2_b_cproj", gate=None)
MLP0 = dict(w1="L0_fc1_w", b1="L0_fc1_b", w2="L0_fc2_w", b2="L0_fc2_b", gate=M_L0 + 5)
MLP2 = dict(w1="L2_W_mlp1", b1="L2_b_mlp1", w2="L2_W_mlp2", b2="L2_b_mlp2", gate=M_L2 + 5)
LOOSE, TIGHT = 0, 1


ATTEND = [("turn", n) for n in range(TURNS + 2)]


def norm(eps, how):
    return [("rows", None), ("stats", eps), ("cols", how)]


STEPS = (
    [("load", None)]
    + norm(TIGHT, (M_L0 + 1, M_L0)) + [("qkv", SELF0), *ATTEND, ("out", SELF0)]
    + norm(TIGHT, "plain") + [("qkv", CROSS0), *ATTEND, ("out", CROSS0)]
    + norm(TIGHT, (M_L0 + 4, M_L0 + 3)) + [("fc1", MLP0), ("fc2", MLP0)]
    + norm(LOOSE, (M_L1Q, M_L1Q + 1)) + [("kvnorm", (LOOSE, (M_L1KV, M_L1KV + 1))), ("qkv", CROSS1),
                                         *ATTEND, ("out", CROSS1)]
    + norm(TIGHT, (M_L2 + 1, M_L2)) + [("qkv", SELF2), *ATTEND, ("out", SELF2)]
    + norm(TIGHT, "plain") + [("kvnorm", (TIGHT, "plain")), ("qkv", CROSS2), *ATTEND, ("out", CROSS2)]
    + norm(TIGHT, (M_L2 + 4, M_L2 + 3)) + [("fc1", MLP2), ("fc2", MLP2)]
    + norm(LOOSE, "affine") + [("l3_qkv", None), ("l3_scores", None), ("l3_evidence", None), ("l3_router", None),
                               ("l3_hidden", None), ("l3_experts", None), ("l3_out", None), ("store", None)]
)
SKEW = 7
ORDER = [(*STEPS[n - SKEW * s], s) for n in range(len(STEPS) + SKEW * (STREAMS - 1))
         for s in range(STREAMS) if 0 <= n - SKEW * s < len(STEPS)]


def bank_uses(kind, arg):
    modulated = isinstance(arg[1] if kind == "kvnorm" else arg, tuple)
    return {
        "load": (1, 1, 0), "rows": (0, 1, 0), "cols": (1, 0, 0) if modulated else (0, 1, 0),
        "kvnorm": (1, 0, 0) if modulated else (0, 1, 0), "qkv": (1, 2, 0),
        "turn": (0, int(kind == "turn" and 1 <= arg <= TURNS), int(kind == "turn" and arg < TURNS)),
        "out": (1, 1, 0), "fc1": (0, 2, 0), "fc2": (1, 0, 0), "l3_qkv": (0, 3, 0), "l3_scores": (0, 0, 1),
        "l3_evidence": (0, 3, 0), "l3_router": (1, 0, 0), "l3_hidden": (0, EXPERTS + 1, 0),
        "l3_experts": (EXPERTS, 1, 0), "l3_out": (1, 1, 0), "store": (0, 1, 0),
    }.get(kind, (0, 0, 0))


USED = np.cumsum([bank_uses(kind, arg) for kind, arg, _ in ORDER], axis=0)
FOR_VECTOR, FOR_SCALAR, OF_SCORES = range(3)


def used_by(n, ring, back=0):
    s = ORDER[n][2]
    while back:
        n -= 1
        back -= ORDER[n][2] == s
    return int(USED[n][ring])


class Counted:

    def __init__(self, eng):
        self.eng, self.seen = eng, {}

    def next(self, sem, by=1):
        self.seen[sem.name] = self.seen.get(sem.name, 0) + by
        self.eng.wait_ge(sem, self.seen[sem.name])
        return self.seen[sem.name]


class Banks:

    def __init__(self, banks, filled, emptied):
        self.banks, self.filled, self.emptied = banks, filled, emptied


class Filler:

    def __init__(self, eng, ring):
        self.eng, self.ring, self.uses = eng, ring, 0

    def slot(self):
        n = len(self.ring.banks)
        if self.uses >= n:
            self.eng.wait_ge(self.ring.emptied, self.uses - n + 1)
        self.uses += 1
        return self.ring.banks[(self.uses - 1) % n]

    def moved_out(self):
        return self.ring.emptied, self.uses


class Emptier:

    def __init__(self, eng, ring):
        self.eng, self.ring, self.uses = eng, ring, 0

    def take(self):
        self.uses += 1
        self.eng.wait_ge(self.ring.filled, self.uses)
        return self.ring.banks[(self.uses - 1) % len(self.ring.banks)]


def build(nc, x, cond, context, weights, biases, rows, ident_in, jmask_in, out):
    B = x.shape[0]
    LOOPS = B // (GROUP * STREAMS)
    assert LOOPS * GROUP * STREAMS == B

    with ExitStack() as ctx:
        def sb(name, shape, dt=F32):
            return ctx.enter_context(nc.sbuf_tensor(name, shape, dt))

        def each(name, shape, dt=F32):
            return [sb(f"{name}{i}", shape, dt) for i in range(STREAMS)]

        def sem(name):
            return ctx.enter_context(nc.semaphore(name))

        w_sb = sb("w_sb", [D, W_COLS])
        b_sb = sb("b_sb", [D, B_COLS])
        row_sb = sb("row_sb", [D, EXPERTS * D + EXPERTS])
        ident = sb("ident_sb", [D, D])
        jmask = sb("jmask_sb", [D, 4])
        eps = sb("eps", [D, 2, 2])
        minus_half = sb("minus_half", [D, 2])
        mods = sb("mods", [D, N_MODS, B])
        cond_rows = sb("cond_rows", [B, D])
        cond_silu = sb("cond_silu", [D, B])

        x_rows, c_rows = each("x_rows", [D, 2, D]), each("c_rows", [D, 2, D])
        xT, cT = each("xT", [D, GROUP, SEQ]), each("cT", [D, GROUP, SEQ])
        nT, kvT = each("nT", [D, GROUP, SEQ]), each("kvT", [D, GROUP, SEQ])
        mod = each("mod", [D, N_MODS, GROUP])
        stats, moments = each("stats", [D, 2, 6]), each("moments", [D, 2, 2])
        c_stats, c_moments = each("c_stats", [D, 2, 6]), each("c_moments", [D, 2, 2])
        shifted, rstd = each("shifted", [D, 2]), each("rstd", [D, 2])
        c_shifted, c_rstd = each("c_shifted", [D, 2, 2]), each("c_rstd", [D, 2, 2])
        r_rows, n_rows = each("r_rows", [D, 2, D]), each("n_rows", [D, 2, D])
        q_heads = each("q_heads", [D, GROUP, 4, SEQ])
        kT = each("kT", [D, GROUP, SEQ])
        v_heads = each("v_heads", [D, 2, HEADS, 2, HD + 1])
        top, denom = each("top", [D, 2, 8]), each("denom", [D, 2 * HEADS])
        o_rows, oT = each("o_rows", [D, 2, D]), each("oT", [D, GROUP, SEQ])
        added = each("added", [D, GROUP, SEQ])
        p_exp, pT = each("p_exp", [D, 2, 512]), each("pT", [D, 2, 4, 2, SEQ])
        hidden = [q[:, :, :, :].rearrange("p g j q -> p g (j q)") for q in q_heads]
        q3, v3 = each("q3", [D, GROUP, SEQ]), each("v3", [D, 2, D])
        top3, total3, inv3 = each("top3", [D, 2]), each("total3", [D, 2]), each("inv3", [D, 2])
        p3, pn3, p3T = each("p3", [D, 2, SEQ]), each("pn3", [D, 2, SEQ]), each("p3T", [D, 2, SEQ])
        evT = each("evT", [D, GROUP, SEQ])
        logits, top_r, probs = each("logits", [D, 2, EXPERTS]), each("top_r", [D, 2]), each("probs", [D, 2, EXPERTS])
        exp_r, total_r, inv_r = each("exp_r", [D, 2, EXPERTS]), each("total_r", [D, 2]), each("inv_r", [D, 2])
        b2_part, b2_mix = each("b2_part", [D, EXPERTS, D]), each("b2_mix", [D, 2, D])
        e_hidden = [[p_exp[s][:, 0, :], p_exp[s][:, 1, :], pT[s][:, 0, :, :, :].rearrange("p c l q -> p (c l q)")]
                    for s in range(STREAMS)]
        g_hidden = [pT[s][:, 1, 0:2, :, :].rearrange("p c l q -> p (c l q)") for s in range(STREAMS)]
        gate, routed, y_rows = kvT, o_rows, x_rows

        bank = [ctx.enter_context(nc.psum_tensor(f"bank{i}", [D, 512], F32)) for i in range(8)]

        first_sem = sem("weights_in")
        weights_in = first_sem
        consts_made = sem("consts_made")
        small_in = sem("small_in")
        cond_moved, mods_filled, mods_moved = sem("cond_moved"), sem("mods_filled"), sem("mods_moved")
        x_in, c_in = [sem(f"x_in{s}") for s in range(STREAMS)], [sem(f"c_in{s}") for s in range(STREAMS)]
        v_filled, v_emptied = sem("v_filled"), sem("v_emptied")
        a_filled, a_emptied = sem("a_filled"), sem("a_emptied")
        s_filled, s_emptied = sem("s_filled"), sem("s_emptied")
        own = sem("own")
        pool_own = sem("pool_own")
        mod_in = sem("mod_in")
        x_added = [sem(f"x_added{s}") for s in range(STREAMS)]
        moments_in, rows_normed = sem("moments_in"), [sem(f"rows_normed{s}") for s in range(STREAMS)]
        c_moments_in = sem("c_moments_in")
        n_modulated = sem("n_modulated")
        kv_modulated = sem("kv_modulated")
        p_done, pv_done = [sem(f"p_done{s}") for s in range(STREAMS)], [sem(f"pv_done{s}") for s in range(STREAMS)]
        o_filled, o_emptied = sem("o_filled"), sem("o_emptied")
        p3_done, p3_normed = sem("p3_done"), sem("p3_normed")
        logits_in, exp_r_in, probs_in, b2_mixed = sem("logits_in"), sem("exp_r_in"), sem("probs_in"), sem("b2_mixed")
        stored = sem("stored")
        last_sem = stored

        to_vector = Banks(bank[0:2], v_filled, v_emptied)
        to_scalar = Banks(bank[2:4], a_filled, a_emptied)
        attended = Banks(bank[4:6], o_filled, o_emptied)
        scores = Banks(bank[6:8], s_filled, s_emptied)

        def w(name, chunk=0, block=0, cols=D):
            at = W_AT[name] + chunk * WEIGHTS[name][1] + block * cols
            return w_sb[:, at:at + cols]

        def bias(name, col=0):
            return b_sb[:, B_AT[name] + col:B_AT[name] + col + 1]

        def over_tokens(ap):
            return ap.unsqueeze(2).broadcast_to([ap.shape[0], ap.shape[1], SEQ])

        def bank4(b):
            return b[:, 0:TOK].rearrange("p (g q) -> p g q", g=GROUP)

        def bank2(b):
            return b[:, 0:2 * D].rearrange("p (t c) -> p t c", t=2)

        with nc.Block() as block:

            @block.sync
            def _(sp):
                sp.dma_start(cond_rows[:, :], cond).then_inc(small_in, 16)
                sp.dma_start(ident[:, :], ident_in).then_inc(small_in, 16)
                sp.dma_start(b_sb[:, :], biases).then_inc(small_in, 16)
                sp.dma_start(w_sb[:, 0:2048], weights[:, 0:2048]).then_inc(small_in, 16)
                sp.dma_start(jmask[:, :], jmask_in).then_inc(weights_in, 16)
                sp.dma_start(row_sb[:, :], rows).then_inc(weights_in, 16)
                sp.dma_start(w_sb[:, 2048:W_COLS], weights[:, 2048:W_COLS]).then_inc(weights_in, 16)
                sp.wait_ge(weights_in, 48)

            @block.gpsimd
            def _(pool):
                nc.gpsimd.memset(eps[:, LOOSE, :], 1e-5).then_inc(consts_made, 1)
                nc.gpsimd.memset(eps[:, TIGHT, :], 1e-6).then_inc(consts_made, 1)
                nc.gpsimd.memset(minus_half[:, :], -0.5).then_inc(consts_made, 1)
                for s in range(STREAMS):
                    pool.wait_ge(consts_made, 3 + 3 * s)
                    nc.gpsimd.memset(v_heads[s][:, :, :, :, :], 0.0).then_inc(consts_made, 1)
                    pool.wait_ge(consts_made, 4 + 3 * s)
                    for b in range(2):
                        nc.gpsimd.memset(v_heads[s][SEQ * b:SEQ * (b + 1), :, :, b, HD:HD + 1], 1.0).then_inc(consts_made, 1)

            @block.tensor
            def _(pe):
                pe.wait_ge(small_in, 64)
                nc.tensor.transpose(bank[0][:, 0:B], cond_rows[:, :], ident[0:B, 0:B]).then_inc(mods_filled, 1)
                pe.wait_ge(cond_moved, 2)
                pe.wait_ge(weights_in, 48)
                for n in range(M_COND):
                    if n >= 4:
                        pe.wait_ge(mods_moved, n - 3)
                    dst = bank[n % 4][:, 0:B]
                    if n < M_EXPERT:
                        name, _, block_, _, _, _ = MODS[n]
                        mm = nc.tensor.matmul(dst, w(name, 0, block_), cond_silu[:, :], start=True, stop=True)
                    elif n < M_GATE:
                        e, r = divmod(n - M_EXPERT, 2)
                        mm = nc.tensor.matmul(dst, w("L3_e_w1", 3 * e + 2, 2 * 0 + r), mods[:, M_COND, :], start=True, stop=True)
                    else:
                        mm = nc.tensor.matmul(dst, w("L3_gate_w1", 2), mods[:, M_COND, :], start=True, stop=True)
                    mm.then_inc(mods_filled, 1)

            @block.scalar
            def _(act):
                act.wait_ge(mods_filled, 1)
                nc.scalar.activation(cond_silu[:, :], bank[0][:, 0:B], ACT.Silu).then_inc(cond_moved, 1)

            @block.vector
            def _(dve):
                dve.wait_ge(cond_moved, 1)
                nc.vector.tensor_copy(mods[:, M_COND, :], bank[0][:, 0:B]).then_inc(cond_moved, 1)
                for n in range(M_COND):
                    dve.wait_ge(mods_filled, n + 2)
                    src = bank[n % 4][:, 0:B]
                    if n < M_EXPERT:
                        _, _, _, name, col, plus = MODS[n]
                    else:
                        name, col, plus = ("L3_e_b1", n - M_EXPERT, False) if n < M_GATE else ("L3_gate_b1", 0, False)
                    nc.vector.tensor_scalar(mods[:, n, :], src, bias(name, col), 1.0 if plus else 0.0,
                                            ALU.add, ALU.add).then_inc(mods_moved, 1)

        nc.multi_engine_barrier(ENGINES, sems_to_clear=range(first_sem.num, last_sem.num + 1))

        with nc.Fori(0, LOOPS) as i:
            with nc.Block() as block:

                @block.sync
                def _(sp):
                    for s in range(STREAMS):
                        at = i * (GROUP * STREAMS) + GROUP * s
                        sp.dma_start(x_rows[s][:, :, :], x[bass.ds(at, GROUP)].rearrange("(t b) q d -> (b q) t d", t=2)).then_inc(x_in[s], 16)
                        sp.dma_start(c_rows[s][:, :, :], context[bass.ds(at, GROUP)].rearrange("(t b) q d -> (b q) t d", t=2)).then_inc(c_in[s], 16)
                    for n, (kind, _, s) in enumerate(ORDER):
                        if kind != "store":
                            continue
                        at = i * (GROUP * STREAMS) + GROUP * s
                        sp.wait_ge(a_emptied, used_by(n, FOR_SCALAR))
                        sp.dma_start(out[bass.ds(at, GROUP)].rearrange("(t b) q d -> (b q) t d", t=2), y_rows[s][:, :, :]).then_inc(stored, 16)
                    sp.wait_ge(stored, 16 * STREAMS)

                @block.gpsimd
                def _(pool):
                    count = Counted(pool)

                    def reciprocal_root(shift, dst, src, e):
                        nc.gpsimd.tensor_tensor(shift, src, eps[:, e, :], ALU.add).then_inc(pool_own, 1)
                        count.next(pool_own)
                        nc.gpsimd.tensor_tensor(dst, shift, minus_half[:, :], ALU.pow).then_inc(pool_own, 1)
                        count.next(pool_own)

                    def normalise(s, src, m, r):
                        for t in range(2):
                            last = nc.gpsimd.tensor_scalar(n_rows[s][:, t, :], src[s][:, t, :], m[:, t, 0:1], r[:, t:t + 1],
                                                           ALU.subtract, ALU.mult)
                        last.then_inc(rows_normed[s], 1)

                    for n, (kind, arg, s) in enumerate(ORDER):
                        if kind == "load":
                            count.next(c_moments_in)
                            for e in (LOOSE, TIGHT):
                                reciprocal_root(c_shifted[s][:, e, :], c_rstd[s][:, e, :], c_moments[s][:, :, 1], e)
                        if kind == "stats":
                            count.next(moments_in)
                            reciprocal_root(shifted[s][:, :], rstd[s][:, :], moments[s][:, :, 1], arg)
                            normalise(s, r_rows, moments[s], rstd[s])
                        if kind == "kvnorm":
                            if arg[0] == LOOSE:
                                pool.wait_ge(v_filled, used_by(n, FOR_VECTOR, back=1))
                            else:
                                pool.wait_ge(a_filled, used_by(n, FOR_SCALAR, back=1))
                            normalise(s, c_rows, c_moments[s], c_rstd[s][:, arg[0], :])
                        if kind == "l3_router":
                            count.next(probs_in)
                            for t in range(2):
                                for e in range(EXPERTS):
                                    nc.gpsimd.tensor_scalar(b2_part[s][:, e, :], row_sb[:, e * D:(e + 1) * D],
                                                            probs[s][:, t, e:e + 1], None, ALU.mult).then_inc(pool_own, 1)
                                count.next(pool_own, EXPERTS)
                                nc.gpsimd.tensor_tensor(b2_mix[s][:, t, :], b2_part[s][:, 0, :], b2_part[s][:, 1, :],
                                                        ALU.add).then_inc(pool_own, 1)
                                count.next(pool_own)
                                nc.gpsimd.tensor_tensor(b2_mix[s][:, t, :], b2_mix[s][:, t, :], b2_part[s][:, 2, :],
                                                        ALU.add).then_inc(b2_mixed if t else pool_own, 1)
                                if not t:
                                    count.next(pool_own)

                @block.tensor
                def _(pe):
                    count = Counted(pe)
                    to_v, to_a, to_s = Filler(pe, to_vector), Filler(pe, to_scalar), Filler(pe, scores)
                    to_o, o_bank = Filler(pe, attended), {}
                    ready = {}

                    def after(what, s):
                        pe.wait_ge(*ready[what, s])

                    def transpose2(dst, src, filled):
                        for t in range(2):
                            mm = nc.tensor.transpose(dst[:, t * D:(t + 1) * D], src(t), ident[:, :])
                        mm.then_inc(filled, 1)

                    for n, (kind, arg, s) in enumerate(ORDER):
                        if kind == "load":
                            pe.wait_ge(x_in[s], 16)
                            transpose2(to_v.slot(), lambda t: x_rows[s][:, t, :], v_filled)
                            ready["x", s] = to_v.moved_out()
                            pe.wait_ge(c_in[s], 16)
                            transpose2(to_a.slot(), lambda t: c_rows[s][:, t, :], a_filled)
                            ready["ctx", s] = to_a.moved_out()

                        if kind == "rows":
                            after("x", s)
                            transpose2(to_a.slot(), lambda t: xT[s][:, 2 * t:2 * t + 2, :], a_filled)

                        if kind == "cols":
                            count.next(rows_normed[s])
                            if isinstance(arg, tuple):
                                transpose2(to_v.slot(), lambda t: n_rows[s][:, t, :], v_filled)
                                ready["n", s] = (n_modulated, count.seen.setdefault("n", 0) + 1)
                                count.seen["n"] += 1
                            else:
                                transpose2(to_a.slot(), lambda t: n_rows[s][:, t, :], a_filled)
                                ready["n", s] = to_a.moved_out()

                        if kind == "kvnorm":
                            count.next(rows_normed[s])
                            if isinstance(arg[1], tuple):
                                transpose2(to_v.slot(), lambda t: n_rows[s][:, t, :], v_filled)
                                ready["kvn", s] = (kv_modulated, s + 1)
                            else:
                                transpose2(to_a.slot(), lambda t: n_rows[s][:, t, :], a_filled)
                                ready["kvn", s] = to_a.moved_out()

                        if kind == "qkv":
                            after("n", s)
                            after(arg["kv"], s)
                            src = {"n": nT, "ctx": cT, "kvn": kvT}[arg["kv"]][s]
                            nc.tensor.matmul(to_v.slot()[:, 0:TOK], w(arg["wq"][0], 0, arg["wq"][1]), nT[s][:, :, :],
                                             start=True, stop=True).then_inc(v_filled, 1)
                            ready["q", s] = to_v.moved_out()
                            nc.tensor.matmul(to_a.slot()[:, 0:TOK], w(arg["wk"][0], 0, arg["wk"][1]), src[:, :, :],
                                             start=True, stop=True).then_inc(a_filled, 1)
                            ready["k", s] = to_a.moved_out()
                            dst = to_a.slot()
                            for t in range(2):
                                mm = nc.tensor.matmul(dst[:, t * D:(t + 1) * D], src[:, 2 * t:2 * t + 2, :],
                                                      w(arg["wv"][0], 0, arg["wv"][1]), start=True, stop=True)
                            mm.then_inc(a_filled, 1)
                            ready["v", s] = to_a.moved_out()

                        if kind == "turn":
                            if arg < TURNS:
                                g = arg
                                if g == 0:
                                    after("q", s)
                                    after("k", s)
                                dst = to_s.slot()
                                part = slice(32 * g, 32 * g + 32)
                                for tb in range(GROUP):
                                    t, b = divmod(tb, 2)
                                    for pair in range(2):
                                        at = ((t * 2 + pair) * 2 + b) * SEQ
                                        mm = nc.tensor.matmul(dst[:, at:at + SEQ], q_heads[s][part, tb, 2 * pair:2 * pair + 2, :],
                                                              kT[s][part, tb, :], start=True, stop=True)
                                mm.then_inc(s_filled, 1)
                            if 1 <= arg <= TURNS:
                                g = arg - 1
                                count.next(p_done[s])
                                dst = to_a.slot()
                                for c in range(4):
                                    mm = nc.tensor.transpose(dst[:, c * D:(c + 1) * D], p_exp[s][:, g % 2, c * D:(c + 1) * D], ident[:, :])
                                mm.then_inc(a_filled, 1)
                                ready["pT", s, g] = to_a.moved_out()
                            if arg >= 2:
                                g = arg - 2
                                if g == 0:
                                    after("v", s)
                                    o_bank[s] = to_o.slot()
                                    ready["o", s] = to_o.moved_out()
                                pe.wait_ge(*ready["pT", s, g])
                                for t in range(2):
                                    for j in range(4):
                                        h = 4 * g + j
                                        mm = nc.tensor.matmul(
                                            o_bank[s][SEQ * t:SEQ * (t + 1), h * O_COLS:(h + 1) * O_COLS],
                                            pT[s][:, g % 2, 2 * t + j // 2, j % 2, :], v_heads[s][:, t, h, :, :],
                                            start=True, stop=True)
                                if g < 2:
                                    mm.then_inc(pv_done[s], 1)
                                elif g == TURNS - 1:
                                    mm.then_inc(o_filled, 1)

                        if kind == "out":
                            after("o", s)
                            transpose2(to_a.slot(), lambda b: o_rows[s][:, b, :], a_filled)
                            pe.wait_ge(*to_a.moved_out())
                            nc.tensor.matmul(to_v.slot()[:, 0:TOK], w(arg["wp"]), oT[s][:, :, :],
                                             start=True, stop=True).then_inc(v_filled, 1)
                            if arg["gate"] is None:
                                ready["x", s] = to_v.moved_out()
                            else:
                                count.seen["x", s] = count.seen.get(("x", s), 0) + 1
                                ready["x", s] = (x_added[s], count.seen["x", s])

                        if kind == "fc1":
                            after("n", s)
                            for half in range(2):
                                dst = to_a.slot()
                                for c in range(2):
                                    mm = nc.tensor.matmul(dst[:, c * TOK:(c + 1) * TOK], w(arg["w1"], 0, 2 * half + c), nT[s][:, :, :],
                                                          start=True, stop=True)
                                mm.then_inc(a_filled, 1)
                            ready["h", s] = to_a.moved_out()

                        if kind == "fc2":
                            after("h", s)
                            dst = to_v.slot()
                            for c in range(4):
                                mm = nc.tensor.matmul(dst[:, 0:TOK], w(arg["w2"], c), hidden[s][:, c, :], start=c == 0, stop=c == 3)
                            mm.then_inc(v_filled, 1)
                            count.seen["x", s] = count.seen.get(("x", s), 0) + 1
                            ready["x", s] = (x_added[s], count.seen["x", s])

                        if kind == "l3_qkv":
                            after("n", s)
                            nc.tensor.matmul(to_a.slot()[:, 0:TOK], w("L3_Wq"), nT[s][:, :, :], start=True, stop=True).then_inc(a_filled, 1)
                            nc.tensor.matmul(to_a.slot()[:, 0:TOK], w("L3_Wk"), cT[s][:, :, :], start=True, stop=True).then_inc(a_filled, 1)
                            dst = to_a.slot()
                            for tb in range(GROUP):
                                t, b = divmod(tb, 2)
                                mm = nc.tensor.matmul(dst[SEQ * t:SEQ * (t + 1), b * D:(b + 1) * D], cT[s][:, tb, :], w("L3_Wv"),
                                                      start=True, stop=True)
                            mm.then_inc(a_filled, 1)
                            ready["qkv3", s] = to_a.moved_out()

                        if kind == "l3_scores":
                            after("qkv3", s)
                            dst = to_s.slot()
                            for tb in range(GROUP):
                                t, b = divmod(tb, 2)
                                mm = nc.tensor.matmul(dst[SEQ * b:SEQ * (b + 1), SEQ * t:SEQ * (t + 1)], q3[s][:, tb, :], kT[s][:, tb, :],
                                                      start=True, stop=True)
                            mm.then_inc(s_filled, 1)

                        if kind == "l3_evidence":
                            count.next(p3_normed)
                            nc.tensor.transpose(to_a.slot()[:, 0:D], pn3[s][:, :, :], ident[:, :]).then_inc(a_filled, 1)
                            pe.wait_ge(*to_a.moved_out())
                            for t in range(2):
                                dst = to_a.slot()
                                part = slice(SEQ * t, SEQ * (t + 1))
                                for b in range(2):
                                    mm = nc.tensor.matmul(dst[:, b * SEQ:(b + 1) * SEQ], v3[s][part, b, :], p3T[s][part, b, :],
                                                          start=True, stop=True)
                                mm.then_inc(a_filled, 1)
                            ready["ev", s] = to_a.moved_out()

                        if kind == "l3_router":
                            after("ev", s)
                            dst = to_v.slot()
                            for tb in range(GROUP):
                                t, b = divmod(tb, 2)
                                parts = [nT[s][:, tb, :], evT[s][:, tb, :], mod[s][:, M_COND, tb:tb + 1].broadcast_to([D, SEQ])]
                                for c in range(3):
                                    at = W_AT["L3_router_W"] + c * EXPERTS
                                    mm = nc.tensor.matmul(dst[SEQ * b:SEQ * (b + 1), t * EXPERTS:(t + 1) * EXPERTS], parts[c],
                                                          w_sb[:, at:at + EXPERTS], start=c == 0, stop=c == 2)
                            mm.then_inc(v_filled, 1)

                        if kind == "l3_hidden":
                            for e in range(EXPERTS):
                                dst = to_a.slot()
                                for r in range(2):
                                    for c, src in enumerate((nT[s], evT[s])):
                                        mm = nc.tensor.matmul(dst[:, r * TOK:(r + 1) * TOK], w("L3_e_w1", 3 * e + c, r), src[:, :, :],
                                                              start=c == 0, stop=c == 1)
                                mm.then_inc(a_filled, 1)
                            ready["eh", s] = to_a.moved_out()
                            dst = to_a.slot()
                            for c, src in enumerate((nT[s], evT[s])):
                                mm = nc.tensor.matmul(dst[:, 0:TOK], w("L3_gate_w1", c), src[:, :, :], start=c == 0, stop=c == 1)
                            mm.then_inc(a_filled, 1)
                            ready["gh", s] = to_a.moved_out()

                        if kind == "l3_experts":
                            after("eh", s)
                            for e in range(EXPERTS):
                                dst = to_v.slot()
                                for t in range(2):
                                    for r in range(2):
                                        mm = nc.tensor.matmul(dst[:, t * D:(t + 1) * D], e_hidden[s][e][:, r * TOK + t * D:r * TOK + (t + 1) * D],
                                                              w("L3_e_w2", 2 * e + r), start=r == 0, stop=r == 1)
                                mm.then_inc(v_filled, 1)
                            ready["routed", s] = to_v.moved_out()
                            after("gh", s)
                            nc.tensor.matmul(to_a.slot()[:, 0:TOK], w("L3_gate_w2"), g_hidden[s], start=True, stop=True).then_inc(a_filled, 1)

                        if kind == "l3_out":
                            after("routed", s)
                            transpose2(to_a.slot(), lambda t: routed[s][:, t, :], a_filled)
                            pe.wait_ge(*to_a.moved_out())
                            nc.tensor.matmul(to_v.slot()[:, 0:TOK], w("L3_out_w"), oT[s][:, :, :], start=True, stop=True).then_inc(v_filled, 1)
                            count.seen["x", s] = count.seen.get(("x", s), 0) + 1
                            ready["x", s] = (x_added[s], count.seen["x", s])

                        if kind == "store":
                            after("x", s)
                            transpose2(to_a.slot(), lambda t: xT[s][:, 2 * t:2 * t + 2, :], a_filled)

                @block.vector
                def _(dve):
                    count = Counted(dve)
                    banks, score_banks = Emptier(dve, to_vector), Emptier(dve, scores)
                    o_banks = Emptier(dve, attended)

                    def own_result(ins):
                        ins.then_inc(own, 1)
                        count.next(own)

                    def add_gated(s, src, b, gate_ap):
                        nc.vector.scalar_tensor_tensor(out=added[s][:, :, :], in0=bank4(src), scalar=b, in1=gate_ap,
                                                       op0=ALU.add, op1=ALU.mult).then_inc(v_emptied, 1)
                        dve.wait_ge(v_emptied, banks.uses)
                        nc.vector.tensor_tensor(xT[s][:, :, :], xT[s][:, :, :], added[s][:, :, :], ALU.add).then_inc(x_added[s], 1)

                    for n, (kind, arg, s) in enumerate(ORDER):
                        if kind == "load":
                            at = i * (GROUP * STREAMS) + GROUP * s
                            nc.vector.tensor_copy(mod[s][:, :, :], mods[:, :, bass.ds(at, GROUP)]).then_inc(mod_in, 1)
                            dve.wait_ge(c_in[s], 16)
                            for t in range(2):
                                own_result(nc.vector.bn_stats(c_stats[s][:, t, :], c_rows[s][:, t, :]))
                            for t in range(2):
                                m = nc.vector.bn_aggr(c_moments[s][:, t, :], c_stats[s][:, t, :])
                            m.then_inc(c_moments_in, 1)
                            src = banks.take()
                            nc.vector.tensor_copy(xT[s][:, :, :], bank4(src)).then_inc(v_emptied, 1)
                            dve.wait_ge(mod_in, s + 1)

                        if kind == "stats":
                            dve.wait_ge(a_emptied, used_by(n, FOR_SCALAR, back=1))
                            for t in range(2):
                                m = nc.vector.bn_stats(stats[s][:, t, :], r_rows[s][:, t, :])
                            own_result(m)
                            for t in range(2):
                                m = nc.vector.bn_aggr(moments[s][:, t, :], stats[s][:, t, :])
                            m.then_inc(moments_in, 1)

                        if kind == "cols" and isinstance(arg, tuple):
                            src = banks.take()
                            nc.vector.tensor_tensor(added[s][:, :, :], bank4(src), over_tokens(mod[s][:, arg[0], :]), ALU.mult).then_inc(v_emptied, 1)
                            dve.wait_ge(v_emptied, banks.uses)
                            nc.vector.tensor_tensor(nT[s][:, :, :], added[s][:, :, :], over_tokens(mod[s][:, arg[1], :]), ALU.add).then_inc(n_modulated, 1)

                        if kind == "kvnorm":
                            if isinstance(arg[1], tuple):
                                src = banks.take()
                                nc.vector.tensor_tensor(added[s][:, :, :], bank4(src), over_tokens(mod[s][:, arg[1][0], :]), ALU.mult).then_inc(v_emptied, 1)
                                dve.wait_ge(v_emptied, banks.uses)
                                nc.vector.tensor_tensor(kvT[s][:, :, :], added[s][:, :, :], over_tokens(mod[s][:, arg[1][1], :]),
                                                        ALU.add).then_inc(kv_modulated, 1)

                        if kind == "qkv":
                            src = banks.take()
                            for j in range(4):
                                m = nc.vector.tensor_scalar(q_heads[s][:, :, j, :], bank4(src), bias(*arg["bq"]), jmask[:, j:j + 1],
                                                            ALU.add, ALU.mult)
                            m.then_inc(v_emptied, 1)

                        if kind == "turn" and arg < TURNS:
                            src = score_banks.take()[:, :].rearrange("p (c k) -> p c k", k=SEQ)
                            own_result(nc.vector.tensor_reduce(top[s][:, arg % 2, :], src, AX.X, ALU.max))
                            nc.vector.tensor_tensor(p_exp[s][:, arg % 2, :].rearrange("p (c k) -> p c k", k=SEQ), src,
                                                    over_tokens(top[s][:, arg % 2, :]), ALU.subtract).then_inc(s_emptied, 1)

                        if kind == "turn" and arg == TURNS + 1:
                            o = o_banks.take()[:, 0:HEADS * O_COLS].rearrange("p (n e) -> p n e", e=HD + 1)
                            own_result(nc.vector.reciprocal(denom[s][:, :], o[:, :, HD:HD + 1].rearrange("p n e -> p (n e)")))
                            nc.vector.tensor_tensor(
                                o_rows[s][:, :, :].rearrange("p b (h d) -> p h b d", h=HEADS),
                                o[:, :, 0:HD].rearrange("p (h b) d -> p h b d", b=2),
                                denom[s][:, :].rearrange("p (h b) -> p h b", b=2).unsqueeze(3).broadcast_to([D, HEADS, 2, HD]),
                                ALU.mult).then_inc(o_emptied, 1)

                        if kind == "out" or kind == "fc2":
                            src = banks.take()
                            b = bias(arg["bp"] if kind == "out" else arg["b2"])
                            if arg["gate"] is None:
                                nc.vector.scalar_tensor_tensor(out=xT[s][:, :, :], in0=bank4(src), scalar=b, in1=xT[s][:, :, :],
                                                               op0=ALU.add, op1=ALU.add).then_inc(v_emptied, 1)
                            else:
                                add_gated(s, src, b, over_tokens(mod[s][:, arg["gate"], :]))

                        if kind == "l3_scores":
                            src = score_banks.take()[:, 0:D].rearrange("p (t k) -> p t k", t=2)
                            own_result(nc.vector.tensor_reduce(top3[s][:, :], src, AX.X, ALU.max))
                            nc.vector.tensor_tensor(p3[s][:, :, :], src, over_tokens(top3[s][:, :]), ALU.subtract).then_inc(s_emptied, 1)

                        if kind == "l3_evidence":
                            count.next(p3_done)
                            own_result(nc.vector.tensor_reduce(total3[s][:, :], p3[s][:, :, :], AX.X, ALU.add))
                            own_result(nc.vector.reciprocal(inv3[s][:, :], total3[s][:, :]))
                            nc.vector.tensor_tensor(pn3[s][:, :, :], p3[s][:, :, :], over_tokens(inv3[s][:, :]), ALU.mult).then_inc(p3_normed, 1)

                        if kind == "l3_router":
                            src = banks.take()
                            bias_row = row_sb[:, EXPERTS * D:EXPERTS * D + EXPERTS].unsqueeze(1).broadcast_to([D, 2, EXPERTS])

                            def over_experts(ap):
                                return ap.unsqueeze(2).broadcast_to([D, 2, EXPERTS])

                            nc.vector.tensor_tensor(logits[s][:, :, :], src[:, 0:2 * EXPERTS].rearrange("p (t e) -> p t e", t=2), bias_row,
                                                    ALU.add).then_inc(v_emptied, 1)
                            dve.wait_ge(v_emptied, banks.uses)
                            own_result(nc.vector.tensor_reduce(top_r[s][:, :], logits[s][:, :, :], AX.X, ALU.max))
                            nc.vector.tensor_tensor(logits[s][:, :, :], logits[s][:, :, :], over_experts(top_r[s][:, :]),
                                                    ALU.subtract).then_inc(logits_in, 1)
                            count.next(exp_r_in)
                            own_result(nc.vector.tensor_reduce(total_r[s][:, :], exp_r[s][:, :, :], AX.X, ALU.add))
                            own_result(nc.vector.reciprocal(inv_r[s][:, :], total_r[s][:, :]))
                            nc.vector.tensor_tensor(probs[s][:, :, :], exp_r[s][:, :, :], over_experts(inv_r[s][:, :]),
                                                    ALU.mult).then_inc(probs_in, 1)

                        if kind == "l3_experts":
                            count.next(b2_mixed)
                            for e in range(EXPERTS):
                                src = banks.take()
                                if e:
                                    dve.wait_ge(v_emptied, banks.uses - 1)
                                for t in range(2):
                                    m = nc.vector.scalar_tensor_tensor(out=routed[s][:, t, :], in0=src[:, t * D:(t + 1) * D],
                                                                       scalar=probs[s][:, t, e:e + 1],
                                                                       in1=(routed if e else b2_mix)[s][:, t, :],
                                                                       op0=ALU.mult, op1=ALU.add)
                                m.then_inc(v_emptied, 1)

                        if kind == "l3_out":
                            add_gated(s, banks.take(), bias("L3_out_b"), gate[s][:, :, :])

                @block.scalar
                def _(act):
                    count = Counted(act)
                    banks = Emptier(act, to_scalar)

                    def move(dst, src, **how):
                        return nc.scalar.activation(dst, src, ACT.Identity, **how).then_inc(a_emptied, 1)

                    for n, (kind, arg, s) in enumerate(ORDER):
                        if kind == "load":
                            move(cT[s][:, :, :], bank4(banks.take()))

                        if kind == "rows":
                            move(r_rows[s][:, :, :], bank2(banks.take()))

                        if kind == "cols" and not isinstance(arg, tuple):
                            if arg == "plain":
                                move(nT[s][:, :, :], bank4(banks.take()))
                            else:
                                move(nT[s][:, :, :], bank4(banks.take()), scale=bias("L3_ln_gamma"), bias=bias("L3_ln_beta"))

                        if kind == "kvnorm" and not isinstance(arg[1], tuple):
                            move(kvT[s][:, :, :], bank4(banks.take()))

                        if kind == "qkv":
                            move(kT[s][:, :, :], bank4(banks.take()), bias=bias(*arg["bk"]))
                            src = banks.take()
                            for b in range(2):
                                part = slice(SEQ * b, SEQ * (b + 1))
                                m = nc.scalar.activation(v_heads[s][part, :, :, b, 0:HD],
                                                         src[part, 0:2 * D].rearrange("p (t h d) -> p t h d", t=2, h=HEADS), ACT.Identity)
                            m.then_inc(a_emptied, 1)

                        if kind == "turn" and arg < TURNS:
                            act.wait_ge(s_emptied, used_by(n, OF_SCORES))
                            nc.scalar.activation(p_exp[s][:, arg % 2, :], p_exp[s][:, arg % 2, :], ACT.Exp,
                                                 scale=ATT_SCALE).then_inc(p_done[s], 1)
                        if kind == "turn" and 1 <= arg <= TURNS:
                            g = arg - 1
                            src = banks.take()
                            if g >= 2:
                                count.next(pv_done[s])
                            move(pT[s][:, g % 2, :, :, :], src[:, :].rearrange("p (c l q) -> p c l q", c=4, l=2))

                        if kind == "out":
                            src = bank2(banks.take()).rearrange("p b (t q) -> p b t q", t=2)
                            move(oT[s][:, :, :].rearrange("p (t b) q -> p b t q", t=2), src, bias=bias(*arg["bv"]))

                        if kind == "fc1":
                            for half in range(2):
                                src = banks.take()
                                for c in range(2):
                                    m = nc.scalar.activation(hidden[s][:, 2 * half + c, :], src[:, c * TOK:(c + 1) * TOK],
                                                             ACT.Gelu_apprx_tanh, bias=bias(arg["b1"], 2 * half + c))
                                m.then_inc(a_emptied, 1)

                        if kind == "l3_qkv":
                            move(q3[s][:, :, :], bank4(banks.take()))
                            move(kT[s][:, :, :], bank4(banks.take()))
                            move(v3[s][:, :, :], bank2(banks.take()))

                        if kind == "l3_scores":
                            act.wait_ge(s_emptied, used_by(n, OF_SCORES))
                            nc.scalar.activation(p3[s][:, :, :], p3[s][:, :, :], ACT.Exp, scale=L3_SCALE).then_inc(p3_done, 1)

                        if kind == "l3_evidence":
                            move(p3T[s][:, :, :], banks.take()[:, 0:D].rearrange("p (b q) -> p b q", b=2))
                            for t in range(2):
                                move(evT[s][:, 2 * t:2 * t + 2, :], banks.take()[:, 0:D].rearrange("p (b q) -> p b q", b=2))

                        if kind == "l3_router":
                            count.next(logits_in)
                            nc.scalar.activation(exp_r[s][:, :, :], logits[s][:, :, :], ACT.Exp).then_inc(exp_r_in, 1)

                        if kind == "l3_hidden":
                            for e in range(EXPERTS + 1):
                                src = banks.take()
                                for r in range(2 if e < EXPERTS else 1):
                                    for tb in range(GROUP):
                                        at = slice(tb * SEQ, (tb + 1) * SEQ)
                                        dst = (e_hidden[s][e][:, r * TOK + tb * SEQ:r * TOK + (tb + 1) * SEQ] if e < EXPERTS
                                               else g_hidden[s][:, at])
                                        k = M_EXPERT + 2 * e + r
                                        m = nc.scalar.activation(dst, src[:, r * TOK + tb * SEQ:r * TOK + (tb + 1) * SEQ], ACT.Silu,
                                                                 bias=mod[s][:, k, tb:tb + 1])
                                m.then_inc(a_emptied, 1)

                        if kind == "l3_experts":
                            src = banks.take()
                            m = nc.scalar.activation(gate[s][:, :, :], bank4(src), ACT.Sigmoid, bias=bias("L3_gate_b2"))
                            m.then_inc(a_emptied, 1)

                        if kind == "l3_out":
                            move(oT[s][:, :, :], bank4(banks.take()))

                        if kind == "store":
                            src = banks.take()
                            move(y_rows[s][:, :, :], bank2(src))

            nc.multi_engine_barrier(ENGINES, sems_to_clear=range(first_sem.num, last_sem.num + 1))


def blocks(a, chunks):
    a = a.reshape(chunks, D, a.shape[-1])
    return a.transpose(1, 0, 2).reshape(D, -1)


def lay_out(inputs):
    g = {k.replace("_xcond", ""): v for k, v in inputs.items()}
    weights = np.concatenate([blocks(g[n], c) for n, (c, _) in WEIGHTS.items()], axis=1)
    biases = np.concatenate([g[n].reshape(c, D).T for n, c in BIASES.items()], axis=1)
    row = np.concatenate([g["L3_e_b2"].reshape(-1), g["L3_router_b"].reshape(-1)])
    return {
        "x": np.ascontiguousarray(g["x"]), "cond": np.ascontiguousarray(g["cond_1024"]),
        "context": np.ascontiguousarray(g["ctx_1024"]),
        "weights": np.ascontiguousarray(weights), "biases": np.ascontiguousarray(biases),
        "rows": np.ascontiguousarray(np.broadcast_to(row, (D, row.size))),
        "ident": np.eye(D, dtype=np.float32),
        "jmask": (np.arange(D)[:, None] // HD % 4 == np.arange(4)[None, :]).astype(np.float32),
    }


def kernel(**inputs):
    import concourse.bacc as bacc
    from concourse.bass_utils import run_bass_kernel_spmd

    nc = bacc.Bacc("TRN2", target_bir_lowering=False, num_devices=1)
    arrays = lay_out({k: np.asarray(v) for k, v in inputs.items()})
    aps = [nc.dram_tensor(n, a.shape, mybir.dt.from_np(a.dtype), kind="ExternalInput").ap() for n, a in arrays.items()]
    out = nc.dram_tensor("out", arrays["x"].shape, F32, kind="ExternalOutput").ap()
    build(nc, *aps, out)
    result = run_bass_kernel_spmd(nc, [arrays], core_ids=[0])
    return result.results[0]["out"]
```

```python
from contextlib import ExitStack

import numpy as np

import concourse.bass as bass
from concourse import mybir

ALU = mybir.AluOpType
ACT = mybir.ActivationFunctionType
AX = mybir.AxisListType
F32 = mybir.dt.float32
ENGINES = [mybir.EngineType.Pool, mybir.EngineType.Activation, mybir.EngineType.PE,
           mybir.EngineType.DVE, mybir.EngineType.SP]

D = 128
HEADS = 16
HD = D // HEADS
SEQ = 64
GROUP = 4
TOK = GROUP * SEQ
STREAMS = 4
ROUNDS = 2
TURNS = HEADS // 4
EXPERTS = 3

WEIGHTS = {
    "L0_adaln_w": (1, 768), "L1_Wss_q": (1, 256), "L1_Wss_kv": (1, 256), "L2_W_mod": (1, 768),
    "L0_qkv_w": (1, 384), "L0_sa_proj_w": (1, 128), "L0_q_w": (1, 128), "L0_kv_w": (1, 256),
    "L0_ca_proj_w": (1, 128), "L0_fc1_w": (1, 512), "L0_fc2_w": (4, 128),
    "L1_Wq": (1, 128), "L1_Wkv": (1, 256), "L1_Wp": (1, 128),
    "L2_W_qkv": (1, 384), "L2_W_proj": (1, 128), "L2_W_qc": (1, 128), "L2_W_kvc": (1, 256),
    "L2_W_cproj": (1, 128), "L2_W_mlp1": (1, 512), "L2_W_mlp2": (4, 128),
    "L3_Wq": (1, 128), "L3_Wk": (1, 128), "L3_Wv": (1, 128), "L3_router_W": (3, 3),
    "L3_e_w1": (9, 256), "L3_e_w2": (6, 128), "L3_gate_w1": (3, 128), "L3_gate_w2": (1, 128),
    "L3_out_w": (1, 128),
}
BIASES = {
    "L0_adaln_b": 6, "L1_bss_q": 2, "L1_bss_kv": 2, "L2_b_mod": 6,
    "L0_qkv_b": 3, "L0_sa_proj_b": 1, "L0_q_b": 1, "L0_kv_b": 2, "L0_ca_proj_b": 1, "L0_fc1_b": 4,
    "L0_fc2_b": 1, "L1_bq": 1, "L1_bkv": 2, "L1_bp": 1,
    "L2_b_qkv": 3, "L2_b_proj": 1, "L2_b_qc": 1, "L2_b_kvc": 2, "L2_b_cproj": 1, "L2_b_mlp1": 4,
    "L2_b_mlp2": 1, "L3_ln_gamma": 1, "L3_ln_beta": 1, "L3_e_b1": 6, "L3_gate_b1": 1,
    "L3_gate_b2": 1, "L3_out_b": 1,
}


def offsets(table, width):
    at, out = 0, {}
    for name, size in table.items():
        out[name] = at
        at += width(size)
    return out, at


W_AT, W_COLS = offsets(WEIGHTS, lambda s: s[0] * s[1])
B_AT, B_COLS = offsets(BIASES, lambda s: s)

ROWS = {
    "L3_e_b2": EXPERTS * D, "L3_router_b": EXPERTS, "L0_fc2_b": D, "L2_b_mlp2": D, "L3_out_b": D, "L3_gate_b2": D,
    "L0_sa_proj_b": D, "L0_ca_proj_b": D, "L1_bp": D, "L2_b_proj": D, "L2_b_cproj": D, "L0_adaln_b": 6 * D, "L2_b_mod": 6 * D,
}
R_AT, R_COLS = offsets(ROWS, lambda n: n)
R_KEPT = R_AT["L0_adaln_b"]

MODS = (
    [("L0_adaln_w", 0, c, "L0_adaln_b", c, c in (1, 4)) for c in (0, 1, 3, 4)]
    + [("L1_Wss_q", 0, c, "L1_bss_q", c, c == 0) for c in range(2)]
    + [("L1_Wss_kv", 0, c, "L1_bss_kv", c, c == 0) for c in range(2)]
    + [("L2_W_mod", 0, c, "L2_b_mod", c, c in (1, 4)) for c in (0, 1, 3, 4)]
)
M_L0, M_L1Q, M_L1KV, M_L2 = 0, 4, 6, 8
GATES = [("L0_adaln_w", 2, "L0_adaln_b"), ("L0_adaln_w", 5, "L0_adaln_b"), ("L2_W_mod", 2, "L2_b_mod"), ("L2_W_mod", 5, "L2_b_mod")]
M_EXPERT = len(MODS)
M_GATE = M_EXPERT + 2 * EXPERTS
M_COND = M_GATE + 1
N_MODS = M_COND + 1

ATT_SCALE = float(HD) ** -0.5
L3_SCALE = float(D) ** -0.5
QUAD = 4 * HD

SELF0 = dict(kv="n", wq=("L0_qkv_w", 0), wk=("L0_qkv_w", 1), wv=("L0_qkv_w", 2), bq=("L0_qkv_b", 0),
             bk=("L0_qkv_b", 1), bv=("L0_qkv_b", 2), wp="L0_sa_proj_w", bp="L0_sa_proj_b", gate=0)
CROSS0 = dict(kv="ctx", wq=("L0_q_w", 0), wk=("L0_kv_w", 0), wv=("L0_kv_w", 1), bq=("L0_q_b", 0),
              bk=("L0_kv_b", 0), bv=("L0_kv_b", 1), wp="L0_ca_proj_w", bp="L0_ca_proj_b", gate=None)
CROSS1 = dict(kv="kvn", wq=("L1_Wq", 0), wk=("L1_Wkv", 0), wv=("L1_Wkv", 1), bq=("L1_bq", 0),
              bk=("L1_bkv", 0), bv=("L1_bkv", 1), wp="L1_Wp", bp="L1_bp", gate=None)
SELF2 = dict(kv="n", wq=("L2_W_qkv", 0), wk=("L2_W_qkv", 1), wv=("L2_W_qkv", 2), bq=("L2_b_qkv", 0),
             bk=("L2_b_qkv", 1), bv=("L2_b_qkv", 2), wp="L2_W_proj", bp="L2_b_proj", gate=2)
CROSS2 = dict(kv="kvn", wq=("L2_W_qc", 0), wk=("L2_W_kvc", 0), wv=("L2_W_kvc", 1), bq=("L2_b_qc", 0),
              bk=("L2_b_kvc", 0), bv=("L2_b_kvc", 1), wp="L2_W_cproj", bp="L2_b_cproj", gate=None)
MLP0 = dict(w1="L0_fc1_w", b1="L0_fc1_b", w2="L0_fc2_w", b2="L0_fc2_b", gate=1)
MLP2 = dict(w1="L2_W_mlp1", b1="L2_b_mlp1", w2="L2_W_mlp2", b2="L2_b_mlp2", gate=3)
LOOSE, TIGHT = 0, 1


ATTENTIONS = [SELF0, CROSS0, CROSS1, SELF2, CROSS2]


def attention(a):
    turns = [("scores", 0)]
    for g in range(1, TURNS):
        turns += [("scores", g), ("keys", g - 1)]
    return [("q", a), ("k", a), ("v", a), *turns, ("keys", TURNS - 1), ("sums", None), ("values", None), ("out", a)]


def mlp(m):
    return [("fc1", (m, 0)), ("fc1", (m, 1)), ("fc2", m)]


def norm(eps, how):
    return [("stats", eps), ("normal", None), ("cols", how)]


GROUP_STEPS = (
    [("load", None), *norm(TIGHT, (M_L0 + 1, M_L0))[:-1], ("context", None), ("cols", (M_L0 + 1, M_L0))] + attention(SELF0)
    + norm(TIGHT, "plain") + attention(CROSS0)
    + norm(TIGHT, (M_L0 + 3, M_L0 + 2)) + mlp(MLP0)
    + norm(LOOSE, (M_L1Q, M_L1Q + 1)) + [("kvnorm", (LOOSE, (M_L1KV, M_L1KV + 1)))] + attention(CROSS1)
    + norm(TIGHT, (M_L2 + 1, M_L2)) + attention(SELF2)
    + norm(TIGHT, "plain") + [("kvnorm", (TIGHT, "plain"))] + attention(CROSS2)
    + norm(TIGHT, (M_L2 + 3, M_L2 + 2)) + mlp(MLP2)
    + norm(LOOSE, "affine") + [("l3_qkv", None), ("l3_scores", None), ("l3_softmax", None), ("l3_keys", None),
                               ("l3_evidence", None), ("l3_router", None), ("l3_probs", None)]
    + [("l3_hidden", EXPERTS), ("l3_hidden", 0), ("l3_hidden", 1), ("l3_experts", EXPERTS), ("l3_hidden", 2)]
    + [("l3_experts", e) for e in range(EXPERTS)]
    + [("l3_cols", None), ("l3_out", None), ("store", None)]
)
STEPS = GROUP_STEPS * ROUNDS

SEQUENCE = (
    "0001000100001101010120120101201220130221311320213320312103201321023032130123012330120213201320101323"
    "0123012031210321320132103203121002332130102312312310302013203103132301202120312031032210301302012301"
    "1230213021302123021013203120120323310213012023130213021302113023102312010312032132012313001320213232"
    "0130132012300121322313001302132013210320213102301203120312310210321020321303213023121030132312013230"
    "1323031232132302233120213032130013000112101203020131012312012103221133232332323232323323000100100000"
    "1101010120120101201220130221311320231320312013201321023032130123012330120213021320101323012301203121"
    "0321320132103203121030232103102312312310302013203103132301202120132030132210031302120301123021302130"
    "2123021013203120120323310123012023130213021302113023102301210312032132012313020132013232013013201230"
    "0232121303013021132013210320213102301203120312310210322100321303213023121030132312013230132303123213"
    "2322033120213032130013000112101203020131012312012103221133232233232332323323"
)


def interleave():
    done, order = [0] * STREAMS, []
    for s in map(int, SEQUENCE):
        order.append((*STEPS[done[s]], s))
        done[s] += 1
    assert done == [len(STEPS)] * STREAMS
    return order


ORDER = interleave()


def bank_uses(kind, arg):
    modulated = isinstance(arg[1] if kind == "kvnorm" else arg, tuple)
    return {
        "context": (0, 1, 0), "cols": (1, 0, 0) if modulated else (0, 1, 0),
        "kvnorm": (1, 0, 0) if modulated else (0, 1, 0), "q": (1, 0, 0), "k": (0, 1, 0), "v": (0, 1, 0),
        "scores": (0, 0, 1), "keys": (0, 1, 0),
        "out": (1, 0, 0), "fc1": (0, 1, 0), "fc2": (1, 0, 0), "l3_qkv": (0, 3, 0), "l3_scores": (0, 0, 1),
        "l3_keys": (0, 1, 0), "l3_evidence": (0, 2, 0), "l3_router": (1, 0, 0), "l3_hidden": (0, 1, 0),
        "l3_experts": (1, 0, 0), "l3_cols": (0, 1, 0), "l3_out": (1, 0, 0),
    }.get(kind, (0, 0, 0))


USED = np.cumsum([bank_uses(kind, arg) for kind, arg, _ in ORDER], axis=0)
FOR_VECTOR, FOR_SCALAR, OF_SCORES = range(3)


def context_norms():
    found = {}
    for n, (kind, _, s) in enumerate(ORDER):
        if kind == "normal":
            following = [step for step in ORDER[n + 1:] if step[2] == s][1]
            if following[0] == "kvnorm":
                found[n] = following[1][0]
    return found


CONTEXT_NORMS = context_norms()


CONTEXT_NORMS_EACH = len(CONTEXT_NORMS) // (STREAMS * ROUNDS)


def used_by(n, ring, back=0):
    s = ORDER[n][2]
    while back:
        n -= 1
        back -= ORDER[n][2] == s
    return int(USED[n][ring])


def residual_before(n):
    s, last, gated = ORDER[n][2], None, 0
    for m in range(n):
        kind, arg, t = ORDER[m]
        if t == s and kind == "load":
            last = None
        if t == s and kind in ("out", "fc2", "l3_out"):
            last = m
            gated += kind == "l3_out" or arg["gate"] is not None
    return last, gated


def round_of(n):
    return sum(kind == "load" and s == ORDER[n][2] for kind, _, s in ORDER[:n + 1]) - 1


class Counted:

    def __init__(self, eng):
        self.eng, self.seen = eng, {}

    def next(self, sem, by=1):
        self.seen[sem.name] = self.seen.get(sem.name, 0) + by
        self.eng.wait_ge(sem, self.seen[sem.name])
        return self.seen[sem.name]


class Banks:

    def __init__(self, banks, filled, emptied):
        self.banks, self.filled, self.emptied = banks, filled, emptied


class Filler:

    def __init__(self, eng, ring):
        self.eng, self.ring, self.uses = eng, ring, 0

    def slot(self):
        n = len(self.ring.banks)
        if self.uses >= n:
            self.eng.wait_ge(self.ring.emptied, self.uses - n + 1)
        self.uses += 1
        return self.ring.banks[(self.uses - 1) % n]

    def moved_out(self):
        return self.ring.emptied, self.uses


class Emptier:

    def __init__(self, eng, ring):
        self.eng, self.ring, self.uses = eng, ring, 0

    def take(self):
        self.uses += 1
        self.eng.wait_ge(self.ring.filled, self.uses)
        return self.ring.banks[(self.uses - 1) % len(self.ring.banks)]


def build(nc, x, cond, context, weights, biases, rows, ident_in, own_head_in, own_ones_in, gate_store, out):
    B = x.shape[0]
    LOOPS = B // (GROUP * STREAMS * ROUNDS)
    assert LOOPS * GROUP * STREAMS * ROUNDS == B

    with ExitStack() as ctx:
        def sb(name, shape, dt=F32):
            return ctx.enter_context(nc.sbuf_tensor(name, shape, dt))

        def each(name, shape, dt=F32):
            return [sb(f"{name}{i}", shape, dt) for i in range(STREAMS)]

        def sem(name):
            return ctx.enter_context(nc.semaphore(name))

        w_sb = sb("w_sb", [D, W_COLS])
        b_sb = sb("b_sb", [D, B_COLS])
        row_sb = sb("row_sb", [D, R_KEPT])
        ident = sb("ident_sb", [D, D])
        own_head = sb("own_head_sb", [D, 4])
        key_bias = sb("key_bias", [D, len(ATTENTIONS), 2])
        own_ones = sb("own_ones_sb", [D, 2, QUAD])
        eps = sb("eps", [D, 2, 2])
        minus_half = sb("minus_half", [D, 2])
        mods = sb("mods", [D, N_MODS, B])
        cond_rows = sb("cond_rows", [B, D])
        cond_silu = sb("cond_silu", [D, B])

        x_rows, c_rows = each("x_rows", [D, 2, D]), each("c_rows", [D, 2, D])
        lifted = each("lifted", [D, 2, D])
        gates = each("gates", [D, 2, len(GATES), D])
        cT = each("cT", [D, GROUP, SEQ])
        nT, kvT = each("nT", [D, GROUP, SEQ]), each("kvT", [D, GROUP, SEQ])
        mod = each("mod", [D, N_MODS, GROUP])
        stats, moments = each("stats", [D, 2, 6]), each("moments", [D, 2, 2])
        c_stats, c_moments = each("c_stats", [D, 2, 6]), each("c_moments", [D, 2, 2])
        shifted, rstd = each("shifted", [D, 2]), each("rstd", [D, 2])
        c_shifted, c_rstd = each("c_shifted", [D, 2, 2]), each("c_rstd", [D, 2, 2])
        n_rows, cn_rows = each("n_rows", [D, 2, D]), each("cn_rows", [D, 2, D])
        q_heads, k_heads = each("q_heads", [D, GROUP, 2, SEQ]), each("k_heads", [D, GROUP, 2, SEQ])
        v_heads = each("v_heads", [D, GROUP * TURNS, 2 * QUAD])
        top, inv_sum = each("top", [D, 2, 8]), each("inv_sum", [D, TOK])
        oT = each("oT", [D, GROUP, SEQ])
        added = each("added", [D, 2, D])
        p_exp, pT = each("p_exp", [D, 2, 512]), each("pT", [D, TURNS, GROUP, 2, SEQ])
        turn_cols = [p[:, :, :, :, :].rearrange("p n g l q -> p n (g l q)") for p in pT]

        def in_turns(n, at, *shape):
            size = int(np.prod(shape))
            names = "abc"[:len(shape)]
            spec = " ".join(names)
            return [cols[:, n, at:at + size].rearrange(f"p ({spec}) -> p {spec}", **dict(zip(names, shape))) for cols in turn_cols]

        hidden = [p[:, 0:2, :, :, :].rearrange("p n (c g) l q -> p (n c) (g l q)", c=2) for p in pT]
        q3, v3, evT = in_turns(2, 0, GROUP, SEQ), in_turns(2, TOK, 2, D), in_turns(3, 0, GROUP, SEQ)
        kT = [k[:, 0:2, :, :].rearrange("p g l k -> p (g l) k") for k in k_heads]
        top3, total3, inv3 = each("top3", [D, 2]), each("total3", [D, 2]), each("inv3", [D, 2])
        p3 = [i[:, 0:D].rearrange("p (t k) -> p t k", t=2) for i in inv_sum]
        pn3 = [i[:, D:2 * D].rearrange("p (t k) -> p t k", t=2) for i in inv_sum]
        p3T = in_turns(3, TOK, 2, SEQ)
        logits, top_r, probs = each("logits", [D, 2, EXPERTS]), each("top_r", [D, 2]), each("probs", [D, 2, EXPERTS])
        exp_r, total_r, inv_r = each("exp_r", [D, 2, EXPERTS]), each("total_r", [D, 2]), each("inv_r", [D, 2])
        b2_part = [q[:, 0:3, :, :].rearrange("p e l q -> p e (l q)") for q in q_heads]
        b2_mix = [k[:, 2:4, :, :].rearrange("p t l k -> p t (l k)") for k in k_heads]
        e_hidden = [[p_exp[s][:, 0, :], p_exp[s][:, 1, :], turn_cols[s][:, 0, :]] for s in range(STREAMS)]
        g_hidden = [turn_cols[s][:, 1, 0:TOK] for s in range(STREAMS)]
        gate = [k[:, :, :].rearrange("p (t g) q -> p t (g q)", t=2) for k in kvT]
        routed = n_rows
        gate_rows, gate_bias = turn_cols[0][:, 0, :], turn_cols[1][:, 0:3, :].rearrange("p n c -> p (n c)")

        bank = [ctx.enter_context(nc.psum_tensor(f"bank{i}", [D, 512], F32)) for i in range(8)]

        first_sem = sem("weights_in")
        weights_in = first_sem
        consts_made = sem("consts_made")
        small_in = sem("small_in")
        gate_rows_in, gates_stored = sem("gate_rows_in"), sem("gates_stored")
        gates_in = [sem(f"gates_in{s}") for s in range(STREAMS)]
        x_lifted = [sem(f"x_lifted{s}") for s in range(STREAMS)]
        gate_in = [sem(f"gate_in{s}") for s in range(STREAMS)]
        cond_moved, mods_filled, mods_moved = sem("cond_moved"), sem("mods_filled"), sem("mods_moved")
        x_in, c_in = [sem(f"x_in{s}") for s in range(STREAMS)], [sem(f"c_in{s}") for s in range(STREAMS)]
        v_filled, v_emptied = sem("v_filled"), sem("v_emptied")
        a_filled, a_emptied = sem("a_filled"), sem("a_emptied")
        s_filled, s_emptied = sem("s_filled"), sem("s_emptied")
        own = sem("own")
        pool_own = sem("pool_own")
        mod_in = sem("mod_in")
        x_added = [sem(f"x_added{s}") for s in range(STREAMS)]
        moments_in, rstd_in = sem("moments_in"), [sem(f"rstd_in{s}") for s in range(STREAMS)]
        rows_normed, c_normed = [sem(f"rows_normed{s}") for s in range(STREAMS)], [sem(f"c_normed{s}") for s in range(STREAMS)]
        c_moments_in = sem("c_moments_in")
        n_modulated = sem("n_modulated")
        kv_modulated = sem("kv_modulated")
        p_done = [sem(f"p_done{s}") for s in range(STREAMS)]
        o_filled, o_emptied = sem("o_filled"), sem("o_emptied")
        p3_done, p3_normed = [sem(f"p3_done{s}") for s in range(STREAMS)], [sem(f"p3_normed{s}") for s in range(STREAMS)]
        exp_r_in, b2_mixed = [sem(f"exp_r_in{s}") for s in range(STREAMS)], [sem(f"b2_mixed{s}") for s in range(STREAMS)]
        logits_in, probs_in = sem("logits_in"), sem("probs_in")
        stored = [sem(f"stored{s}") for s in range(STREAMS)]
        last_sem = stored[-1]

        to_vector = Banks(bank[0:2], v_filled, v_emptied)
        to_scalar = Banks(bank[2:4], a_filled, a_emptied)
        attended = Banks(bank[4:6], o_filled, o_emptied)
        scores = Banks(bank[6:8], s_filled, s_emptied)

        def w(name, chunk=0, block=0, cols=D):
            at = W_AT[name] + chunk * WEIGHTS[name][1] + block * cols
            return w_sb[:, at:at + cols]

        def bias(name, col=0):
            return b_sb[:, B_AT[name] + col:B_AT[name] + col + 1]

        def row(name):
            at = R_AT[name]
            return row_sb[:, at:at + D].unsqueeze(1).broadcast_to([D, 2, D])

        def x_changed(n):
            last, gated = residual_before(n)
            s = ORDER[n][2]
            if last is None:
                return x_in[s], 16 * (round_of(n) + 1)
            if ORDER[last][0] == "out" and ORDER[last][1]["gate"] is None:
                return v_emptied, used_by(last, FOR_VECTOR)
            return x_added[s], gated

        def over_tokens(ap):
            return ap.unsqueeze(2).broadcast_to([ap.shape[0], ap.shape[1], SEQ])

        def bank4(b):
            return b[:, 0:TOK].rearrange("p (g q) -> p g q", g=GROUP)

        def bank2(b):
            return b[:, 0:2 * D].rearrange("p (t c) -> p t c", t=2)

        with nc.Block() as block:

            @block.sync
            def _(sp):
                sp.dma_start(cond_rows[:, :], cond).then_inc(small_in, 16)
                sp.dma_start(ident[:, :], ident_in).then_inc(small_in, 16)
                sp.dma_start(b_sb[:, :], biases).then_inc(small_in, 16)
                sp.dma_start(w_sb[:, 0:2048], weights[:, 0:2048]).then_inc(small_in, 16)
                sp.dma_start(own_head[:, :], own_head_in).then_inc(small_in, 16)
                sp.dma_start(own_ones[:, :, :], own_ones_in.rearrange("p (l c) -> p l c", l=2)).then_inc(weights_in, 16)
                sp.dma_start(row_sb[:, :], rows[:, 0:R_KEPT]).then_inc(weights_in, 16)
                sp.dma_start(gate_bias[:, 0:R_COLS - R_KEPT], rows[:, R_KEPT:R_COLS]).then_inc(weights_in, 16)
                sp.dma_start(w_sb[:, 2048:W_COLS], weights[:, 2048:W_COLS]).then_inc(weights_in, 16)
                sp.wait_ge(weights_in, 64)
                sp.wait_ge(gate_rows_in, len(GATES))
                sp.dma_start(gate_store, gate_rows[0:B, :]).then_inc(gates_stored, 16)
                sp.wait_ge(gates_stored, 16)

            @block.gpsimd
            def _(pool):
                nc.gpsimd.memset(eps[:, LOOSE, :], 1e-5).then_inc(consts_made, 1)
                nc.gpsimd.memset(eps[:, TIGHT, :], 1e-6).then_inc(consts_made, 1)
                nc.gpsimd.memset(minus_half[:, :], -0.5).then_inc(consts_made, 1)
                for s in range(STREAMS):
                    nc.gpsimd.memset(v_heads[s][:, :, :], 0.0).then_inc(consts_made, 1)

            @block.tensor
            def _(pe):
                pe.wait_ge(small_in, 80)
                nc.tensor.transpose(bank[0][:, 0:B], cond_rows[:, :], ident[0:B, 0:B]).then_inc(mods_filled, 1)
                pe.wait_ge(cond_moved, 2)
                pe.wait_ge(weights_in, 64)
                for n in range(M_COND):
                    if n >= 4:
                        pe.wait_ge(mods_moved, n - 3)
                    dst = bank[n % 4][:, 0:B]
                    if n < M_EXPERT:
                        name, _, block_, _, _, _ = MODS[n]
                        mm = nc.tensor.matmul(dst, w(name, 0, block_), cond_silu[:, :], start=True, stop=True)
                    elif n < M_GATE:
                        e, r = divmod(n - M_EXPERT, 2)
                        mm = nc.tensor.matmul(dst, w("L3_e_w1", 3 * e + 2, 2 * 0 + r), mods[:, M_COND, :], start=True, stop=True)
                    else:
                        mm = nc.tensor.matmul(dst, w("L3_gate_w1", 2), mods[:, M_COND, :], start=True, stop=True)
                    mm.then_inc(mods_filled, 1)
                for n, a in enumerate(ATTENTIONS):
                    mm = nc.tensor.matmul(bank[4 + n // 4][:, n % 4 * D:(n % 4 + 1) * D], bias(*a["bv"]).broadcast_to([D, D]), w(a["wp"]),
                                          start=True, stop=True)
                mm.then_inc(mods_filled, 1)
                for n, (name, block_, _) in enumerate(GATES):
                    mm = nc.tensor.matmul(bank[6][0:B, n * D:(n + 1) * D], cond_silu[:, :], w(name, 0, block_), start=True, stop=True)
                mm.then_inc(mods_filled, 1)

            @block.scalar
            def _(act):
                act.wait_ge(mods_filled, 1)
                nc.scalar.activation(cond_silu[:, :], bank[0][:, 0:B], ACT.Silu).then_inc(cond_moved, 1)

            @block.vector
            def _(dve):
                dve.wait_ge(cond_moved, 1)
                nc.vector.tensor_copy(mods[:, M_COND, :], bank[0][:, 0:B]).then_inc(cond_moved, 1)
                for n in range(M_COND):
                    dve.wait_ge(mods_filled, n + 2)
                    src = bank[n % 4][:, 0:B]
                    if n < M_EXPERT:
                        _, _, _, name, col, plus = MODS[n]
                    else:
                        name, col, plus = ("L3_e_b1", n - M_EXPERT, False) if n < M_GATE else ("L3_gate_b1", 0, False)
                    nc.vector.tensor_scalar(mods[:, n, :], src, bias(name, col), 1.0 if plus else 0.0,
                                            ALU.add, ALU.add).then_inc(mods_moved, 1)
                dve.wait_ge(mods_filled, M_COND + 2)
                for n, a in enumerate(ATTENTIONS):
                    at = R_AT[a["bp"]]
                    nc.vector.tensor_tensor(row_sb[:, at:at + D], row_sb[:, at:at + D], bank[4 + n // 4][:, n % 4 * D:(n % 4 + 1) * D],
                                            ALU.add).then_inc(mods_moved, 1)
                    nc.vector.tensor_scalar(key_bias[:, n, :], own_head[:, 2:4], bias(*a["bk"]), None, ALU.mult).then_inc(mods_moved, 1)
                dve.wait_ge(mods_filled, M_COND + 3)
                for n, (_, block_, name) in enumerate(GATES):
                    at = R_AT[name] - R_KEPT + block_ * D
                    nc.vector.tensor_tensor(gate_rows[0:B, n * D:(n + 1) * D], bank[6][0:B, n * D:(n + 1) * D], gate_bias[0:B, at:at + D],
                                            ALU.add).then_inc(gate_rows_in, 1)

        nc.multi_engine_barrier(ENGINES, sems_to_clear=range(first_sem.num, last_sem.num + 1))

        with nc.Fori(0, LOOPS) as i:
            with nc.Block() as block:

                @block.sync
                def _(sp):
                    def group(s, r):
                        return bass.ds(i * (GROUP * STREAMS * ROUNDS) + GROUP * (STREAMS * r + s), GROUP)

                    def rows_of(ap, s, r):
                        return ap[group(s, r)].rearrange("(t b) q d -> (b q) t d", t=2)

                    def load_gates(s, r):
                        of_b = gate_store[group(s, r)].rearrange("(t b) c -> b t c", t=2)
                        for b in range(2):
                            sp.dma_start(gates[s][SEQ * b:SEQ * (b + 1), :, :, :].rearrange("p t n c -> p t (n c)"),
                                         of_b[b].unsqueeze(0).broadcast_to([SEQ, 2, len(GATES) * D])).then_inc(gates_in[s], 16)

                    for s in range(STREAMS):
                        sp.dma_start(x_rows[s][:, :, :], rows_of(x, s, 0)).then_inc(x_in[s], 16)
                        sp.dma_start(c_rows[s][:, :, :], rows_of(context, s, 0)).then_inc(c_in[s], 16)
                    for s in range(STREAMS):
                        load_gates(s, 0)
                    for n, (kind, _, s) in enumerate(ORDER):
                        if kind == "l3_qkv" and round_of(n) + 1 < ROUNDS:
                            r = round_of(n)
                            sp.wait_ge(c_normed[s], CONTEXT_NORMS_EACH * (r + 1))
                            sp.dma_start(c_rows[s][:, :, :], rows_of(context, s, r + 1)).then_inc(c_in[s], 16)
                            sp.wait_ge(*x_changed(n))
                            load_gates(s, r + 1)
                        if kind == "store":
                            r = round_of(n)
                            sp.wait_ge(*x_changed(n))
                            sp.dma_start(rows_of(out, s, r), x_rows[s][:, :, :]).then_inc(stored[s], 16)
                            sp.wait_ge(stored[s], 16 * (r + 1))
                            if r + 1 < ROUNDS:
                                sp.dma_start(x_rows[s][:, :, :], rows_of(x, s, r + 1)).then_inc(x_in[s], 16)

                @block.gpsimd
                def _(pool):
                    count = Counted(pool)

                    def reciprocal_root(shift, dst, src, e, done=pool_own):
                        nc.gpsimd.tensor_tensor(shift, src, eps[:, e, :], ALU.add).then_inc(pool_own, 1)
                        count.next(pool_own)
                        nc.gpsimd.tensor_tensor(dst, shift, minus_half[:, :], ALU.pow).then_inc(done, 1)
                        if done is pool_own:
                            count.next(pool_own)

                    for n, (kind, arg, s) in enumerate(ORDER):
                        if kind == "context":
                            count.next(c_moments_in)
                            for e in (LOOSE, TIGHT):
                                reciprocal_root(c_shifted[s][:, e, :], c_rstd[s][:, e, :], c_moments[s][:, :, 1], e)
                        if kind == "stats":
                            count.next(moments_in)
                            reciprocal_root(shifted[s][:, :], rstd[s][:, :], moments[s][:, :, 1], arg, rstd_in[s])
                        if kind == "normal" and n in CONTEXT_NORMS:
                            eps_at = CONTEXT_NORMS[n]
                            for t in range(2):
                                m = nc.gpsimd.tensor_scalar(cn_rows[s][:, t, :], c_rows[s][:, t, :], c_moments[s][:, t, 0:1],
                                                            c_rstd[s][:, eps_at, t:t + 1], ALU.subtract, ALU.mult)
                            m.then_inc(c_normed[s], 1)
                        if kind == "q" or kind == "fc1" and arg[1] == 0:
                            pool.wait_ge(*x_changed(n))
                            layer = arg if kind == "q" else arg[0]
                            b = row(layer["bp" if kind == "q" else "b2"])
                            if layer["gate"] is not None:
                                if layer["gate"] == 0:
                                    pool.wait_ge(gates_in[s], 32 * (round_of(n) + 1))
                                nc.gpsimd.tensor_tensor(lifted[s][:, :, :], gates[s][:, :, layer["gate"], :], b, ALU.mult).then_inc(pool_own, 1)
                                count.next(pool_own)
                                b = lifted[s][:, :, :]
                            nc.gpsimd.tensor_tensor(lifted[s][:, :, :], x_rows[s][:, :, :], b, ALU.add).then_inc(x_lifted[s], 1)
                        if kind == "l3_probs":
                            count.next(probs_in)
                            for t in range(2):
                                for e in range(EXPERTS):
                                    nc.gpsimd.tensor_scalar(b2_part[s][:, e, :], row_sb[:, e * D:(e + 1) * D],
                                                            probs[s][:, t, e:e + 1], None, ALU.mult).then_inc(pool_own, 1)
                                count.next(pool_own, EXPERTS)
                                nc.gpsimd.tensor_tensor(b2_mix[s][:, t, :], b2_part[s][:, 0, :], b2_part[s][:, 1, :],
                                                        ALU.add).then_inc(pool_own, 1)
                                count.next(pool_own)
                                nc.gpsimd.tensor_tensor(b2_mix[s][:, t, :], b2_mix[s][:, t, :], b2_part[s][:, 2, :],
                                                        ALU.add).then_inc(b2_mixed[s] if t else pool_own, 1)
                                if not t:
                                    count.next(pool_own)

                @block.tensor
                def _(pe):
                    count = Counted(pe)
                    to_v, to_a, to_s = Filler(pe, to_vector), Filler(pe, to_scalar), Filler(pe, scores)
                    to_o = Filler(pe, attended)
                    ready = {}

                    def after(what, s):
                        pe.wait_ge(*ready[what, s])

                    def transpose2(dst, src, filled):
                        for t in range(2):
                            mm = nc.tensor.transpose(dst[:, t * D:(t + 1) * D], src(t), ident[:, :])
                        mm.then_inc(filled, 1)

                    def with_bias(dst, src, weight, b):
                        for t in range(2):
                            at = R_AT[b]
                            nc.tensor.matmul(dst[:, t * D:(t + 1) * D], ident[:, :], row_sb[:, at:at + D], start=True, stop=False)
                            mm = nc.tensor.matmul(dst[:, t * D:(t + 1) * D], src(t), w(weight), start=False, stop=True)
                        mm.then_inc(v_filled, 1)

                    for n, (kind, arg, s) in enumerate(ORDER):
                        if kind == "context":
                            pe.wait_ge(c_in[s], 16 * (round_of(n) + 1))
                            transpose2(to_a.slot(), lambda t: c_rows[s][:, t, :], a_filled)
                            ready["ctx", s] = to_a.moved_out()

                        if kind == "cols":
                            count.next(rows_normed[s])
                            if isinstance(arg, tuple):
                                transpose2(to_v.slot(), lambda t: n_rows[s][:, t, :], v_filled)
                                ready["n", s] = (n_modulated, count.seen.setdefault("n", 0) + 1)
                                count.seen["n"] += 1
                            else:
                                transpose2(to_a.slot(), lambda t: n_rows[s][:, t, :], a_filled)
                                ready["n", s] = to_a.moved_out()

                        if kind == "kvnorm":
                            count.next(c_normed[s])
                            if isinstance(arg[1], tuple):
                                transpose2(to_v.slot(), lambda t: cn_rows[s][:, t, :], v_filled)
                                ready["kvn", s] = (kv_modulated, count.seen.setdefault("kv", 0) + 1)
                                count.seen["kv"] += 1
                            else:
                                transpose2(to_a.slot(), lambda t: cn_rows[s][:, t, :], a_filled)
                                ready["kvn", s] = to_a.moved_out()

                        if kind in ("q", "k", "v"):
                            after("n" if kind == "q" else arg["kv"], s)
                            src = {"n": nT, "ctx": cT, "kvn": kvT}[arg["kv"]][s]
                        if kind == "q":
                            nc.tensor.matmul(to_v.slot()[:, 0:TOK], w(arg["wq"][0], 0, arg["wq"][1]), nT[s][:, :, :],
                                             start=True, stop=True).then_inc(v_filled, 1)
                            ready["q", s] = to_v.moved_out()
                        if kind == "k":
                            nc.tensor.matmul(to_a.slot()[:, 0:TOK], w(arg["wk"][0], 0, arg["wk"][1]), src[:, :, :],
                                             start=True, stop=True).then_inc(a_filled, 1)
                            ready["k", s] = to_a.moved_out()
                        if kind == "v":
                            dst = to_a.slot()
                            wv = w(arg["wv"][0], 0, arg["wv"][1]).rearrange("p (g r c) -> p g r c", g=TURNS, r=2)
                            for tb in range(GROUP):
                                for pair in range(2):
                                    mm = nc.tensor.matmul(dst[SEQ * pair:SEQ * (pair + 1), tb * SEQ:(tb + 1) * SEQ], src[:, tb, :],
                                                          wv[:, :, pair, :], start=True, stop=True)
                            mm.then_inc(a_filled, 1)
                            ready["v", s] = to_a.moved_out()

                        if kind == "scores":
                            g = arg
                            if g == 0:
                                after("q", s)
                                after("k", s)
                            dst = to_s.slot()
                            part = slice(32 * g, 32 * g + 32)
                            for tb in range(GROUP):
                                mm = nc.tensor.matmul(dst[:, tb * D:(tb + 1) * D], q_heads[s][part, tb, :, :], k_heads[s][part, tb, :, :],
                                                      start=True, stop=True)
                            mm.then_inc(s_filled, 1)

                        if kind == "keys":
                            g = arg
                            count.next(p_done[s])
                            dst = to_a.slot()
                            for c in range(4):
                                mm = nc.tensor.transpose(dst[:, c * D:(c + 1) * D], p_exp[s][:, g % 2, c * D:(c + 1) * D], ident[:, :])
                            mm.then_inc(a_filled, 1)
                            ready["pT", s] = to_a.moved_out()

                        if kind == "sums":
                            after("pT", s)
                            dst = to_o.slot()
                            for lo in range(2):
                                for g in range(TURNS):
                                    mm = nc.tensor.matmul(dst[QUAD * g:QUAD * (g + 1), 0:TOK], own_ones[:, lo, :], pT[s][:, g, :, lo, :],
                                                          start=lo == 0, stop=lo == 1)
                            mm.then_inc(o_filled, 1)

                        if kind == "values":
                            after("v", s)
                            dst = to_o.slot()
                            ready["o", s] = to_o.moved_out()
                            for tb in range(GROUP):
                                for lo in range(2):
                                    for g in range(TURNS):
                                        mm = nc.tensor.matmul(dst[QUAD * g:QUAD * (g + 1), tb * SEQ:(tb + 1) * SEQ],
                                                              v_heads[s][:, tb * TURNS + g, lo * QUAD:(lo + 1) * QUAD], pT[s][:, g, tb, lo, :],
                                                              start=lo == 0, stop=lo == 1)
                            mm.then_inc(o_filled, 1)

                        if kind == "out":
                            after("o", s)
                            dst = to_v.slot()
                            for t in range(2):
                                mm = nc.tensor.matmul(dst[:, t * D:(t + 1) * D], oT[s][:, 2 * t:2 * t + 2, :], w(arg["wp"]), start=True, stop=True)
                            mm.then_inc(v_filled, 1)

                        if kind == "fc1":
                            after("n", s)
                            dst, (layer, half) = to_a.slot(), arg
                            for c in range(2):
                                mm = nc.tensor.matmul(dst[:, c * TOK:(c + 1) * TOK], w(layer["w1"], 0, 2 * half + c), nT[s][:, :, :],
                                                      start=True, stop=True)
                            mm.then_inc(a_filled, 1)
                            ready["h", s] = to_a.moved_out()

                        if kind == "fc2":
                            after("h", s)
                            dst = to_v.slot()
                            for t in range(2):
                                for c in range(4):
                                    mm = nc.tensor.matmul(dst[:, t * D:(t + 1) * D], hidden[s][:, c, t * D:(t + 1) * D], w(arg["w2"], c),
                                                          start=c == 0, stop=c == 3)
                            mm.then_inc(v_filled, 1)

                        if kind == "l3_qkv":
                            after("n", s)
                            nc.tensor.matmul(to_a.slot()[:, 0:TOK], w("L3_Wq"), nT[s][:, :, :], start=True, stop=True).then_inc(a_filled, 1)
                            nc.tensor.matmul(to_a.slot()[:, 0:TOK], w("L3_Wk"), cT[s][:, :, :], start=True, stop=True).then_inc(a_filled, 1)
                            dst = to_a.slot()
                            for tb in range(GROUP):
                                t, b = divmod(tb, 2)
                                mm = nc.tensor.matmul(dst[SEQ * t:SEQ * (t + 1), b * D:(b + 1) * D], cT[s][:, tb, :], w("L3_Wv"),
                                                      start=True, stop=True)
                            mm.then_inc(a_filled, 1)
                            ready["qkv3", s] = to_a.moved_out()

                        if kind == "l3_scores":
                            after("qkv3", s)
                            dst = to_s.slot()
                            for tb in range(GROUP):
                                t, b = divmod(tb, 2)
                                mm = nc.tensor.matmul(dst[SEQ * b:SEQ * (b + 1), SEQ * t:SEQ * (t + 1)], q3[s][:, tb, :], kT[s][:, tb, :],
                                                      start=True, stop=True)
                            mm.then_inc(s_filled, 1)

                        if kind == "l3_keys":
                            count.next(p3_normed[s])
                            nc.tensor.transpose(to_a.slot()[:, 0:D], pn3[s][:, :, :], ident[:, :]).then_inc(a_filled, 1)
                            ready["p3T", s] = to_a.moved_out()

                        if kind == "l3_evidence":
                            after("p3T", s)
                            for t in range(2):
                                dst = to_a.slot()
                                part = slice(SEQ * t, SEQ * (t + 1))
                                for b in range(2):
                                    mm = nc.tensor.matmul(dst[:, b * SEQ:(b + 1) * SEQ], v3[s][part, b, :], p3T[s][part, b, :],
                                                          start=True, stop=True)
                                mm.then_inc(a_filled, 1)
                            ready["ev", s] = to_a.moved_out()

                        if kind == "l3_router":
                            after("ev", s)
                            dst = to_v.slot()
                            for tb in range(GROUP):
                                t, b = divmod(tb, 2)
                                parts = [nT[s][:, tb, :], evT[s][:, tb, :], mod[s][:, M_COND, tb:tb + 1].broadcast_to([D, SEQ])]
                                for c in range(3):
                                    at = W_AT["L3_router_W"] + c * EXPERTS
                                    mm = nc.tensor.matmul(dst[SEQ * b:SEQ * (b + 1), t * EXPERTS:(t + 1) * EXPERTS], parts[c],
                                                          w_sb[:, at:at + EXPERTS], start=c == 0, stop=c == 2)
                            mm.then_inc(v_filled, 1)

                        if kind == "l3_hidden":
                            dst, e = to_a.slot(), arg
                            for r in range(2 if e < EXPERTS else 1):
                                for c, src in enumerate((nT[s], evT[s])):
                                    weight = w("L3_e_w1", 3 * e + c, r) if e < EXPERTS else w("L3_gate_w1", c)
                                    mm = nc.tensor.matmul(dst[:, r * TOK:(r + 1) * TOK], weight, src[:, :, :], start=c == 0, stop=c == 1)
                            mm.then_inc(a_filled, 1)
                            ready["hidden", s, e] = to_a.moved_out()

                        if kind == "l3_experts" and arg < EXPERTS:
                            dst, e = to_v.slot(), arg
                            pe.wait_ge(*ready["hidden", s, e])
                            for t in range(2):
                                for r in range(2):
                                    mm = nc.tensor.matmul(dst[:, t * D:(t + 1) * D], e_hidden[s][e][:, r * TOK + t * D:r * TOK + (t + 1) * D],
                                                          w("L3_e_w2", 2 * e + r), start=r == 0, stop=r == 1)
                            mm.then_inc(v_filled, 1)
                            ready["routed", s] = to_v.moved_out()

                        if kind == "l3_experts" and arg == EXPERTS:
                            pe.wait_ge(*ready["hidden", s, arg])
                            with_bias(to_v.slot(), lambda t: g_hidden[s][:, t * D:(t + 1) * D], "L3_gate_w2", "L3_gate_b2")

                        if kind == "l3_cols":
                            after("routed", s)
                            transpose2(to_a.slot(), lambda t: routed[s][:, t, :], a_filled)
                            ready["rT", s] = to_a.moved_out()

                        if kind == "l3_out":
                            after("rT", s)
                            with_bias(to_v.slot(), lambda t: oT[s][:, 2 * t:2 * t + 2, :], "L3_out_w", "L3_out_b")

                @block.vector
                def _(dve):
                    count = Counted(dve)
                    banks, score_banks = Emptier(dve, to_vector), Emptier(dve, scores)
                    o_banks, sums_at = Emptier(dve, attended), {}

                    def own_result(ins):
                        ins.then_inc(own, 1)
                        count.next(own)

                    def add_gated(s, src, gate_ap):
                        nc.vector.tensor_tensor(added[s][:, :, :], bank2(src), gate_ap, ALU.mult).then_inc(v_emptied, 1)
                        dve.wait_ge(v_emptied, banks.uses)
                        nc.vector.tensor_tensor(x_rows[s][:, :, :], added[s][:, :, :], lifted[s][:, :, :], ALU.add).then_inc(x_added[s], 1)

                    for n, (kind, arg, s) in enumerate(ORDER):
                        if kind == "load":
                            at = i * (GROUP * STREAMS * ROUNDS) + GROUP * (STREAMS * round_of(n) + s)
                            nc.vector.tensor_copy(mod[s][:, :, :], mods[:, :, bass.ds(at, GROUP)]).then_inc(mod_in, 1)
                            count.next(mod_in)

                        if kind == "context":
                            dve.wait_ge(c_in[s], 16 * (round_of(n) + 1))
                            for t in range(2):
                                own_result(nc.vector.bn_stats(c_stats[s][:, t, :], c_rows[s][:, t, :]))
                            for t in range(2):
                                m = nc.vector.bn_aggr(c_moments[s][:, t, :], c_stats[s][:, t, :])
                            m.then_inc(c_moments_in, 1)

                        if kind == "stats":
                            dve.wait_ge(*x_changed(n))
                            for t in range(2):
                                m = nc.vector.bn_stats(stats[s][:, t, :], x_rows[s][:, t, :])
                            own_result(m)
                            for t in range(2):
                                m = nc.vector.bn_aggr(moments[s][:, t, :], stats[s][:, t, :])
                            m.then_inc(moments_in, 1)

                        if kind == "normal":
                            count.next(rstd_in[s])
                            for t in range(2):
                                m = nc.vector.tensor_scalar(n_rows[s][:, t, :], x_rows[s][:, t, :], moments[s][:, t, 0:1], rstd[s][:, t:t + 1],
                                                            ALU.subtract, ALU.mult)
                            m.then_inc(rows_normed[s], 1)

                        if kind == "cols" and isinstance(arg, tuple):
                            src = banks.take()
                            nc.vector.tensor_tensor(nT[s][:, :, :], bank4(src), over_tokens(mod[s][:, arg[0], :]), ALU.mult).then_inc(v_emptied, 1)
                            dve.wait_ge(v_emptied, banks.uses)
                            nc.vector.tensor_tensor(nT[s][:, :, :], nT[s][:, :, :], over_tokens(mod[s][:, arg[1], :]), ALU.add).then_inc(n_modulated, 1)

                        if kind == "kvnorm":
                            if isinstance(arg[1], tuple):
                                src = banks.take()
                                nc.vector.tensor_tensor(kvT[s][:, :, :], bank4(src), over_tokens(mod[s][:, arg[1][0], :]), ALU.mult).then_inc(v_emptied, 1)
                                dve.wait_ge(v_emptied, banks.uses)
                                nc.vector.tensor_tensor(kvT[s][:, :, :], kvT[s][:, :, :], over_tokens(mod[s][:, arg[1][1], :]),
                                                        ALU.add).then_inc(kv_modulated, 1)

                        if kind == "q":
                            src = banks.take()
                            for lo in range(2):
                                m = nc.vector.tensor_scalar(q_heads[s][:, :, lo, :], bank4(src), bias(*arg["bq"]), own_head[:, lo:lo + 1],
                                                            ALU.add, ALU.mult)
                            m.then_inc(v_emptied, 1)

                        if kind == "scores":
                            src = score_banks.take()[:, :].rearrange("p (c k) -> p c k", k=SEQ)
                            own_result(nc.vector.tensor_reduce(top[s][:, arg % 2, :], src, AX.X, ALU.max))
                            nc.vector.tensor_tensor(p_exp[s][:, arg % 2, :].rearrange("p (c k) -> p c k", k=SEQ), src,
                                                    over_tokens(top[s][:, arg % 2, :]), ALU.subtract).then_inc(s_emptied, 1)

                        if kind == "sums":
                            nc.vector.reciprocal(inv_sum[s][:, :], o_banks.take()[:, 0:TOK]).then_inc(o_emptied, 1)
                            sums_at[s] = o_banks.uses

                        if kind == "values":
                            src = o_banks.take()
                            dve.wait_ge(o_emptied, sums_at[s])
                            nc.vector.tensor_tensor(oT[s][:, :, :].rearrange("p g q -> p (g q)"), src[:, 0:TOK], inv_sum[s][:, :],
                                                    ALU.mult).then_inc(o_emptied, 1)

                        if kind == "out" or kind == "fc2":
                            src = banks.take()
                            count.next(x_lifted[s])
                            if arg["gate"] is None:
                                nc.vector.tensor_tensor(x_rows[s][:, :, :], bank2(src), lifted[s][:, :, :], ALU.add).then_inc(v_emptied, 1)
                            else:
                                if arg["gate"] == 0:
                                    dve.wait_ge(gates_in[s], 32 * (round_of(n) + 1))
                                add_gated(s, src, gates[s][:, :, arg["gate"], :])

                        if kind == "l3_scores":
                            src = score_banks.take()[:, 0:D].rearrange("p (t k) -> p t k", t=2)
                            own_result(nc.vector.tensor_reduce(top3[s][:, :], src, AX.X, ALU.max))
                            nc.vector.tensor_tensor(p3[s][:, :, :], src, over_tokens(top3[s][:, :]), ALU.subtract).then_inc(s_emptied, 1)

                        if kind == "l3_softmax":
                            count.next(p3_done[s])
                            own_result(nc.vector.tensor_reduce(total3[s][:, :], p3[s][:, :, :], AX.X, ALU.add))
                            own_result(nc.vector.reciprocal(inv3[s][:, :], total3[s][:, :]))
                            nc.vector.tensor_tensor(pn3[s][:, :, :], p3[s][:, :, :], over_tokens(inv3[s][:, :]), ALU.mult).then_inc(p3_normed[s], 1)

                        if kind == "l3_router":
                            src = banks.take()
                            at = R_AT["L3_router_b"]
                            bias_row = row_sb[:, at:at + EXPERTS].unsqueeze(1).broadcast_to([D, 2, EXPERTS])

                            def over_experts(ap):
                                return ap.unsqueeze(2).broadcast_to([D, 2, EXPERTS])

                            nc.vector.tensor_tensor(logits[s][:, :, :], src[:, 0:2 * EXPERTS].rearrange("p (t e) -> p t e", t=2), bias_row,
                                                    ALU.add).then_inc(v_emptied, 1)
                            dve.wait_ge(v_emptied, banks.uses)
                            own_result(nc.vector.tensor_reduce(top_r[s][:, :], logits[s][:, :, :], AX.X, ALU.max))
                            nc.vector.tensor_tensor(logits[s][:, :, :], logits[s][:, :, :], over_experts(top_r[s][:, :]),
                                                    ALU.subtract).then_inc(logits_in, 1)

                        if kind == "l3_probs":
                            def over_experts(ap):
                                return ap.unsqueeze(2).broadcast_to([D, 2, EXPERTS])

                            count.next(exp_r_in[s])
                            own_result(nc.vector.tensor_reduce(total_r[s][:, :], exp_r[s][:, :, :], AX.X, ALU.add))
                            own_result(nc.vector.reciprocal(inv_r[s][:, :], total_r[s][:, :]))
                            nc.vector.tensor_tensor(probs[s][:, :, :], exp_r[s][:, :, :], over_experts(inv_r[s][:, :]),
                                                    ALU.mult).then_inc(probs_in, 1)

                        if kind == "l3_experts":
                            src = banks.take()
                            if arg == EXPERTS:
                                nc.vector.tensor_copy(gate[s], bank2(src)).then_inc(v_emptied, 1)
                            else:
                                if arg == 0:
                                    count.next(b2_mixed[s])
                                else:
                                    dve.wait_ge(v_emptied, used_by(n, FOR_VECTOR, back=1))
                                for t in range(2):
                                    m = nc.vector.scalar_tensor_tensor(out=routed[s][:, t, :], in0=src[:, t * D:(t + 1) * D],
                                                                       scalar=probs[s][:, t, arg:arg + 1],
                                                                       in1=(routed if arg else b2_mix)[s][:, t, :],
                                                                       op0=ALU.mult, op1=ALU.add)
                                m.then_inc(v_emptied, 1)

                        if kind == "l3_out":
                            count.next(gate_in[s])
                            src = banks.take()
                            nc.vector.scalar_tensor_tensor(out=added[s][:, :, :], in0=gate[s], scalar=1.0, in1=bank2(src),
                                                           op0=ALU.add, op1=ALU.mult).then_inc(v_emptied, 1)
                            dve.wait_ge(v_emptied, banks.uses)
                            nc.vector.scalar_tensor_tensor(out=x_rows[s][:, :, :], in0=added[s][:, :, :], scalar=0.5, in1=x_rows[s][:, :, :],
                                                           op0=ALU.mult, op1=ALU.add).then_inc(x_added[s], 1)

                @block.scalar
                def _(act):
                    count = Counted(act)
                    banks = Emptier(act, to_scalar)

                    def move(dst, src, **how):
                        return nc.scalar.activation(dst, src, ACT.Identity, **how).then_inc(a_emptied, 1)

                    for n, (kind, arg, s) in enumerate(ORDER):
                        if kind == "context":
                            move(cT[s][:, :, :], bank4(banks.take()))

                        if kind == "cols" and not isinstance(arg, tuple):
                            if arg == "plain":
                                move(nT[s][:, :, :], bank4(banks.take()))
                            else:
                                move(nT[s][:, :, :], bank4(banks.take()), scale=bias("L3_ln_gamma"), bias=bias("L3_ln_beta"))

                        if kind == "kvnorm" and not isinstance(arg[1], tuple):
                            move(kvT[s][:, :, :], bank4(banks.take()))

                        if kind == "k":
                            src, n_att = banks.take(), ATTENTIONS.index(arg)
                            for pair in range(2):
                                m = nc.scalar.activation(k_heads[s][:, :, pair, :], bank4(src), ACT.Identity,
                                                         scale=own_head[:, 2 + pair:3 + pair], bias=key_bias[:, n_att, pair:pair + 1])
                            m.then_inc(a_emptied, 1)
                        if kind == "v":
                            src = banks.take()
                            for pair in range(2):
                                part = slice(SEQ * pair, SEQ * (pair + 1))
                                for lo in range(2):
                                    at = lo * QUAD + (2 * pair + lo) * HD
                                    m = nc.scalar.activation(v_heads[s][part, :, at:at + HD],
                                                             src[part, 0:TOK].rearrange("p (n l d) -> p n l d", l=2, d=HD)[:, :, lo, :],
                                                             ACT.Identity)
                            m.then_inc(a_emptied, 1)

                        if kind == "scores":
                            act.wait_ge(s_emptied, used_by(n, OF_SCORES))
                            nc.scalar.activation(p_exp[s][:, arg % 2, :], p_exp[s][:, arg % 2, :], ACT.Exp,
                                                 scale=ATT_SCALE).then_inc(p_done[s], 1)
                        if kind == "keys":
                            g = arg
                            src = banks.take()
                            move(pT[s][:, g, :, :, :], src[:, :].rearrange("p (c l q) -> p c l q", c=4, l=2))

                        if kind == "fc1":
                            src, (layer, half) = banks.take(), arg
                            for c in range(2):
                                m = nc.scalar.activation(hidden[s][:, 2 * half + c, :], src[:, c * TOK:(c + 1) * TOK],
                                                         ACT.Gelu_apprx_tanh, bias=bias(layer["b1"], 2 * half + c))
                            m.then_inc(a_emptied, 1)

                        if kind == "l3_qkv":
                            move(q3[s][:, :, :], bank4(banks.take()))
                            move(kT[s][:, :, :], bank4(banks.take()))
                            move(v3[s][:, :, :], bank2(banks.take()))

                        if kind == "l3_scores":
                            act.wait_ge(s_emptied, used_by(n, OF_SCORES))
                            nc.scalar.activation(p3[s][:, :, :], p3[s][:, :, :], ACT.Exp, scale=L3_SCALE).then_inc(p3_done[s], 1)

                        if kind == "l3_keys":
                            move(p3T[s][:, :, :], banks.take()[:, 0:D].rearrange("p (b q) -> p b q", b=2))

                        if kind == "l3_evidence":
                            for t in range(2):
                                move(evT[s][:, 2 * t:2 * t + 2, :], banks.take()[:, 0:D].rearrange("p (b q) -> p b q", b=2))

                        if kind == "l3_router":
                            count.next(logits_in)
                            nc.scalar.activation(exp_r[s][:, :, :], logits[s][:, :, :], ACT.Exp).then_inc(exp_r_in[s], 1)

                        if kind == "l3_hidden":
                            src, e = banks.take(), arg
                            for r in range(2 if e < EXPERTS else 1):
                                for tb in range(GROUP):
                                    at = slice(r * TOK + tb * SEQ, r * TOK + (tb + 1) * SEQ)
                                    dst = (e_hidden[s][e] if e < EXPERTS else g_hidden[s])[:, at]
                                    k = M_EXPERT + 2 * e + r
                                    m = nc.scalar.activation(dst, src[:, at], ACT.Silu, bias=mod[s][:, k, tb:tb + 1])
                            m.then_inc(a_emptied, 1)

                        if kind == "l3_experts" and arg == EXPERTS:
                            act.wait_ge(v_emptied, used_by(n, FOR_VECTOR))
                            nc.scalar.activation(gate[s], gate[s], ACT.Tanh, scale=0.5).then_inc(gate_in[s], 1)

                        if kind == "l3_cols":
                            move(oT[s][:, :, :], bank4(banks.take()))

            nc.multi_engine_barrier(ENGINES, sems_to_clear=range(first_sem.num, last_sem.num + 1))


def blocks(a, chunks):
    a = a.reshape(chunks, D, a.shape[-1])
    return a.transpose(1, 0, 2).reshape(D, -1)


def lay_out(inputs):
    g = {k.replace("_xcond", ""): v for k, v in inputs.items()}
    weights = np.concatenate([blocks(g[n], c) for n, (c, _) in WEIGHTS.items()], axis=1)
    biases = np.concatenate([g[n].reshape(c, D).T for n, c in BIASES.items()], axis=1)
    row = np.concatenate([g[n].reshape(-1) for n in ROWS])
    slot = np.arange(D) // HD % 4
    own_head = np.stack([slot % 2 == 0, slot % 2 == 1, slot // 2 == 0, slot // 2 == 1], axis=1).astype(np.float32)
    own_ones = (np.arange(QUAD)[None, None, :] // HD
                == 2 * (np.arange(D)[:, None, None] // SEQ) + np.arange(2)[None, :, None]).astype(np.float32)
    return {
        "x": np.ascontiguousarray(g["x"]), "cond": np.ascontiguousarray(g["cond_1024"]),
        "context": np.ascontiguousarray(g["ctx_1024"]),
        "weights": np.ascontiguousarray(weights), "biases": np.ascontiguousarray(biases),
        "rows": np.ascontiguousarray(np.broadcast_to(row, (D, row.size))),
        "ident": np.eye(D, dtype=np.float32),
        "own_head": own_head,
        "own_ones": own_ones.reshape(D, -1),
    }


def kernel(**inputs):
    import concourse.bacc as bacc
    from concourse.bass_utils import run_bass_kernel_spmd

    nc = bacc.Bacc("TRN2", target_bir_lowering=False, num_devices=1)
    arrays = lay_out({k: np.asarray(v) for k, v in inputs.items()})
    aps = [nc.dram_tensor(n, a.shape, mybir.dt.from_np(a.dtype), kind="ExternalInput").ap() for n, a in arrays.items()]
    out = nc.dram_tensor("out", arrays["x"].shape, F32, kind="ExternalOutput").ap()
    gate_store = nc.dram_tensor("gate_store", (arrays["x"].shape[0], len(GATES) * D), F32, kind="Internal").ap()
    build(nc, *aps, gate_store, out)
    result = run_bass_kernel_spmd(nc, [arrays], core_ids=[0])
    return result.results[0]["out"]
```
